# Optimizing a Trainium2 kernel written in Bass

```python
import numpy as np
import jax
import jax.numpy as jnp

def _softmax(x, axis=-1):
    return jax.nn.softmax(x, axis=axis)

def _gelu(x):
    return jax.nn.gelu(x, approximate=True)

def _silu(x):
    return jax.nn.silu(x)

def _sigmoid(x):
    return jax.nn.sigmoid(x)

def _layernorm(x, axis=-1, eps=1e-05):
    m = jnp.mean(x, axis=axis, keepdims=True)
    v = jnp.var(x, axis=axis, keepdims=True)
    return (x - m) / jnp.sqrt(v + eps)

def _scatter_add(tgt, idx, src, axis=0):
    return tgt.at[idx].add(src)

def _segment_sum(src, seg, n):
    return jax.ops.segment_sum(src, seg, n)
kernel_name = 'mk_vit_tower_d1_tok_img256_r4_84dcd2'

def setup_inputs(seed: int=0):
    np.random.seed(seed)
    _w = jnp.asarray

    def _rec_inputs():
        import jax
        import jax.numpy as jnp
        _rk = jax.random.key(seed)
        x = 7.22013e-05 + 1.00017 * jax.random.normal(jax.random.fold_in(_rk, 1), (8, 64, 64, 64), jnp.float32)
        return x
    x = _rec_inputs()

    def _L0_tok_setup():
        import jax, jax.numpy as jnp
        import numpy as np
        B, C, H, W = (8, 64, 64, 64)
        NB = 3
        E = 64
        key = jax.random.key(seed)
        ks = jax.random.split(key, 6)
        x = jax.random.normal(ks[0], (B, C, H, W), dtype=jnp.float32)
        bases = jax.random.normal(ks[1], (C, NB), dtype=jnp.float32)
        W_spline = jax.random.normal(ks[2], (E, C * NB), dtype=jnp.float32) * (1.0 / np.sqrt(C * NB))
        b_spline = jax.random.normal(ks[3], (E,), dtype=jnp.float32) * 0.01
        W_base = jax.random.normal(ks[4], (E, C), dtype=jnp.float32) * (1.0 / np.sqrt(C))
        b_base = jax.random.normal(ks[5], (E,), dtype=jnp.float32) * 0.01
        return {'x': x, 'bases': bases, 'W_spline': W_spline, 'b_spline': b_spline, 'W_base': W_base, 'b_base': b_base}
    _L0_tok_all = _L0_tok_setup()
    _L0_tok_in = {k: v for k, v in _L0_tok_all.items() if k in ('bases', 'W_spline', 'b_spline', 'W_base', 'b_base')}
    del _L0_tok_all

    def _L0_attn_setup():
        import jax, jax.numpy as jnp
        import numpy as np
        import math
        CHUNK = 128

        def _build_slopes(n):

            def p2(n):
                start = 2.0 ** (-2.0 ** (-(math.log2(n) - 3)))
                return [start ** (i + 1) for i in range(n)]
            if math.log2(n).is_integer():
                s = p2(n)
            else:
                c = 2 ** math.floor(math.log2(n))
                s = p2(c) + p2(2 * c)[0::2][:n - c]
            return np.asarray(s, dtype=np.float32)

        def _lightning_attn(q, k, v, slopes):
            b, h, l, d = q.shape
            n = l // CHUNK
            s = slopes.reshape(h, 1, 1)
            pos = jnp.arange(CHUNK, dtype=q.dtype)
            diff = pos[:, None] - pos[None, :]
            mask = jnp.where(diff >= 0, jnp.exp(-s * diff), 0.0)[None]
            q_dec = jnp.exp(-slopes[:, None] * pos)[None, :, :, None]
            k_dec = jnp.exp(-slopes[:, None] * (CHUNK - pos))[None, :, :, None]
            blk = jnp.exp(-slopes * CHUNK).reshape(1, h, 1, 1)
            qc = q.reshape(b, h, n, CHUNK, d).transpose(2, 0, 1, 3, 4)
            kc = k.reshape(b, h, n, CHUNK, d).transpose(2, 0, 1, 3, 4)
            vc = v.reshape(b, h, n, CHUNK, d).transpose(2, 0, 1, 3, 4)

            def step(S, xs):
                qi, ki, vi = xs
                scores = jnp.einsum('bhcd,bhed->bhce', qi, ki) * mask
                intra = jnp.einsum('bhce,bhed->bhcd', scores, vi)
                inter = jnp.einsum('bhcd,bhde->bhce', qi * q_dec, S)
                S_new = blk * S + jnp.einsum('bhcd,bhce->bhde', ki * k_dec, vi)
                return (S_new, intra + inter)
            S0 = jnp.zeros((b, h, d, d), q.dtype)
            _, o = jax.lax.scan(step, S0, (qc, kc, vc))
            return o.transpose(1, 2, 0, 3, 4).reshape(b, h, l, d)
        key = jax.random.key(seed)
        k1, k2, k3 = jax.random.split(key, 3)
        b, l, c, h = (8, 4096, 64, 8)
        x = jax.random.normal(k1, (b, l, c), dtype=jnp.float32)
        w_qkv = jax.random.normal(k2, (c, 3 * c), dtype=jnp.float32) * 0.02
        w_proj = jax.random.normal(k3, (c, c), dtype=jnp.float32) * 0.02
        b_proj = jnp.zeros((c,), dtype=jnp.float32)
        slopes = jnp.asarray(_build_slopes(h))
        return {'x': x, 'w_qkv': w_qkv, 'w_proj': w_proj, 'b_proj': b_proj, 'slopes': slopes}
    _L0_attn_all = _L0_attn_setup()
    _L0_attn_in = {k: v for k, v in _L0_attn_all.items() if k in ('w_qkv', 'w_proj', 'b_proj', 'slopes')}
    del _L0_attn_all

    def _L0_ffn_setup():
        import jax, jax.numpy as jnp
        import numpy as np
        TOP_K = 2
        key = jax.random.key(seed)
        ks = jax.random.split(key, 4)
        B, L, D, H, E = (8, 1024, 64, 256, 8)
        s = 0.02
        return {'x': jax.random.normal(ks[0], (B, L, D), jnp.float32), 'Wg': jax.random.normal(ks[1], (D, E), jnp.float32) * s, 'bg': jnp.zeros((E,), jnp.float32), 'W1': jax.random.normal(ks[2], (E, D, H), jnp.float32) * s, 'b1': jnp.zeros((E, H), jnp.float32), 'W2': jax.random.normal(ks[3], (E, H, D), jnp.float32) * s, 'b2': jnp.zeros((E, D), jnp.float32)}
    _L0_ffn_all = _L0_ffn_setup()
    _L0_ffn_in = {k: v for k, v in _L0_ffn_all.items() if k in ('Wg', 'bg', 'W1', 'b1', 'W2', 'b2')}
    del _L0_ffn_all
    return {'x': x, 'L0_tok_bases': _L0_tok_in['bases'], 'L0_tok_W_spline': _L0_tok_in['W_spline'], 'L0_tok_b_spline': _L0_tok_in['b_spline'], 'L0_tok_W_base': _L0_tok_in['W_base'], 'L0_tok_b_base': _L0_tok_in['b_base'], 'L0_attn_w_qkv': _L0_attn_in['w_qkv'], 'L0_attn_w_proj': _L0_attn_in['w_proj'], 'L0_attn_b_proj': _L0_attn_in['b_proj'], 'L0_attn_slopes': _L0_attn_in['slopes'], 'L0_ffn_Wg': _L0_ffn_in['Wg'], 'L0_ffn_bg': _L0_ffn_in['bg'], 'L0_ffn_W1': _L0_ffn_in['W1'], 'L0_ffn_b1': _L0_ffn_in['b1'], 'L0_ffn_W2': _L0_ffn_in['W2'], 'L0_ffn_b2': _L0_ffn_in['b2']}

def reference(x, L0_tok_bases, L0_tok_W_spline, L0_tok_b_spline, L0_tok_W_base, L0_tok_b_base, L0_attn_w_qkv, L0_attn_w_proj, L0_attn_b_proj, L0_attn_slopes, L0_ffn_Wg, L0_ffn_bg, L0_ffn_W1, L0_ffn_b1, L0_ffn_W2, L0_ffn_b2):
    import jax
    import jax.numpy as jnp

    def _L0_tok_ref(x, bases, W_spline, b_spline, W_base, b_base):
        import jax, jax.numpy as jnp
        import numpy as np
        B, C, H, W = (8, 64, 64, 64)
        NB = 3
        E = 64
        b, c, h, w = x.shape
        x_flat = jnp.transpose(x.reshape(b, c, h * w), (0, 2, 1))
        base_out = jnp.einsum('blc,ec->ble', jax.nn.silu(x_flat), W_base) + b_base
        spline = jax.nn.sigmoid(x_flat[..., None] * bases[None, None, :, :])
        spline_flat = spline.reshape(b, h * w, c * bases.shape[1])
        spline_proj = jnp.einsum('blk,ek->ble', spline_flat, W_spline) + b_spline
        return base_out + spline_proj

    def _L0_attn_ref(x, w_qkv, w_proj, b_proj, slopes):
        import jax, jax.numpy as jnp
        import numpy as np
        import math
        CHUNK = 128

        def _build_slopes(n):

            def p2(n):
                start = 2.0 ** (-2.0 ** (-(math.log2(n) - 3)))
                return [start ** (i + 1) for i in range(n)]
            if math.log2(n).is_integer():
                s = p2(n)
            else:
                c = 2 ** math.floor(math.log2(n))
                s = p2(c) + p2(2 * c)[0::2][:n - c]
            return np.asarray(s, dtype=np.float32)

        def _lightning_attn(q, k, v, slopes):
            b, h, l, d = q.shape
            n = l // CHUNK
            s = slopes.reshape(h, 1, 1)
            pos = jnp.arange(CHUNK, dtype=q.dtype)
            diff = pos[:, None] - pos[None, :]
            mask = jnp.where(diff >= 0, jnp.exp(-s * diff), 0.0)[None]
            q_dec = jnp.exp(-slopes[:, None] * pos)[None, :, :, None]
            k_dec = jnp.exp(-slopes[:, None] * (CHUNK - pos))[None, :, :, None]
            blk = jnp.exp(-slopes * CHUNK).reshape(1, h, 1, 1)
            qc = q.reshape(b, h, n, CHUNK, d).transpose(2, 0, 1, 3, 4)
            kc = k.reshape(b, h, n, CHUNK, d).transpose(2, 0, 1, 3, 4)
            vc = v.reshape(b, h, n, CHUNK, d).transpose(2, 0, 1, 3, 4)

            def step(S, xs):
                qi, ki, vi = xs
                scores = jnp.einsum('bhcd,bhed->bhce', qi, ki) * mask
                intra = jnp.einsum('bhce,bhed->bhcd', scores, vi)
                inter = jnp.einsum('bhcd,bhde->bhce', qi * q_dec, S)
                S_new = blk * S + jnp.einsum('bhcd,bhce->bhde', ki * k_dec, vi)
                return (S_new, intra + inter)
            S0 = jnp.zeros((b, h, d, d), q.dtype)
            _, o = jax.lax.scan(step, S0, (qc, kc, vc))
            return o.transpose(1, 2, 0, 3, 4).reshape(b, h, l, d)
        b, l, c = x.shape
        h = slopes.shape[0]
        d = c // h
        scale = d ** (-0.5)
        qkv = (x @ w_qkv).reshape(b, l, 3, h, d)
        q = qkv[:, :, 0].transpose(0, 2, 1, 3) * scale
        k = qkv[:, :, 1].transpose(0, 2, 1, 3)
        v = qkv[:, :, 2].transpose(0, 2, 1, 3)
        o = _lightning_attn(q, k, v, slopes)
        out = o.transpose(0, 2, 1, 3).reshape(b, l, c) @ w_proj + b_proj
        return out

    def _L0_ffn_ref(x, Wg, bg, W1, b1, W2, b2):
        import jax, jax.numpy as jnp
        import numpy as np
        TOP_K = 2
        B, L, D = x.shape
        E = W1.shape[0]
        xf = x.reshape(-1, D)
        gate_logits = xf @ Wg + bg
        top_w, top_i = jax.lax.top_k(gate_logits, TOP_K)
        top_w = jax.nn.softmax(top_w, axis=-1)
        w_dense = jnp.sum(jax.nn.one_hot(top_i, E, dtype=xf.dtype) * top_w[..., None], axis=1)
        out = jnp.zeros_like(xf)
        for e in range(E):
            h = jax.nn.gelu(xf @ W1[e] + b1[e], approximate=False)
            out = out + w_dense[:, e:e + 1] * (h @ W2[e] + b2[e])
        return out.reshape(B, L, D)
    h = _L0_tok_ref(x, L0_tok_bases, L0_tok_W_spline, L0_tok_b_spline, L0_tok_W_base, L0_tok_b_base)
    h = h + _L0_attn_ref(_layernorm(h, axis=-1), L0_attn_w_qkv, L0_attn_w_proj, L0_attn_b_proj, L0_attn_slopes)
    h = h + _L0_ffn_ref(_layernorm(h, axis=-1), L0_ffn_Wg, L0_ffn_bg, L0_ffn_W1, L0_ffn_b1, L0_ffn_W2, L0_ffn_b2)
    return h

_drawn_inputs = setup_inputs


def setup_inputs(seed=0):
    import zlib

    import numpy as np

    out = dict(_drawn_inputs(seed))
    spreads = {'L0_attn_b_proj': (0.0, 0.1),
     'L0_ffn_bg': (0.0, 0.1),
     'L0_ffn_b1': (0.0, 0.566),
     'L0_ffn_b2': (0.0, 0.1)}
    factors = {'L0_tok_b_spline': 3.193, 'L0_tok_b_base': 3.152}
    for name, (base, spread) in spreads.items():
        noise = np.random.default_rng([zlib.crc32(name.encode()), seed]).standard_normal(out[name].shape)
        drawn = base * np.exp(spread * noise) if base else spread * noise
        out[name] = jnp.asarray(drawn.astype(out[name].dtype))
    for name, factor in factors.items():
        out[name] = (out[name] * factor).astype(out[name].dtype)
    return out
```

```python
import math
from contextlib import ExitStack

import concourse.bass as bass
from concourse import mybir

F32 = mybir.dt.float32
F32R = mybir.dt.float32r
BF16 = mybir.dt.bfloat16
U32 = mybir.dt.uint32
ALU = mybir.AluOpType
ACT = mybir.ActivationFunctionType

P = 128
IMAGES = 8
TOKENS = 4096
CHUNK = 128
CHUNKS = TOKENS // CHUNK
C = 64
HEADS = 8
D = C // HEADS
EXPERTS = 8
HIDDEN = 256
TILES = 4
GT = TILES * CHUNK
GROUPS = IMAGES * TOKENS // GT
PAIRS = EXPERTS // 2
HALVES = HIDDEN // P
SCALE = float(D) ** -0.5
EPS = 1e-5
Q_PARTS = (0, 0, 1, 0, 2, 1)
K_PARTS = (0, 1, 0, 2, 0, 1)
STACK = len(Q_PARTS) * D

LEAD = 4
LOOPS = (GROUPS - LEAD) // 2 - 1


class Turn:

    def __init__(self, i, c):
        self.i, self.c = i, c

    def back(self, n):
        return Turn(self.i, self.c - n)

    def ahead(self, n):
        return Turn(self.i, self.c + n)

    @property
    def exists(self):
        assert self.i is None or self.c >= 0, "peel more steps before the loop"
        return 0 <= self.c and (self.i is not None or self.c < GROUPS)

    @property
    def slot(self):
        return self.c % 2

    @property
    def chunk(self):
        return self.c // 2 if self.i is None else self.i + self.c // 2

    def count(self, per_group, events=None):
        events = per_group if events is None else events
        if self.i is None:
            return per_group * self.c + events
        return self.i * (2 * per_group) + (per_group * self.c + events)

    def slot_count(self, per_group):
        if self.i is None:
            return per_group * (self.c // 2 + 1)
        return self.i * per_group + per_group * (self.c // 2 + 1)


def build_tower(nc, x, front_w, front_scale, front_bias, wqk, wkv, wproj, bproj, slope_cols, slope_rows,
                wg, bg, w1, b1, w2, b2, identity, distance, causal, position, to_end, same_head,
                expert_numbers, out):
    with ExitStack() as ctx:
        def sb(name, shape, dt=F32):
            return ctx.enter_context(nc.sbuf_tensor(name, shape, dt))

        def sem(name):
            return ctx.enter_context(nc.semaphore(name))

        ident = sb("ident", [P, P])
        front_w_sb = sb("front_w_sb", [P, 2, C])
        front_scale_sb = sb("front_scale_sb", [P, 2])
        front_b_sb = sb("front_b_sb", [P, 1])
        embed_bias = sb("embed_bias", [P, 1])
        spline_rows = sb("spline_rows", [P, 2])
        wqk_sb = sb("wqk_sb", [P, P])
        wkv_sb = sb("wkv_sb", [P, P])
        wqk_part = [sb(f"wqk_part{n}", [P, P], F32R) for n in range(2)]
        wkv_part = [sb(f"wkv_part{n}", [P, P], F32R) for n in range(2)]
        wproj_sb = sb("wproj_sb", [P, P])
        bproj_sb = sb("bproj_sb", [P, C])
        slope_cols_sb = sb("slope_cols_sb", [C, 1])
        slope_rows_sb = sb("slope_rows_sb", [P, HEADS])
        distance_sb = sb("distance_sb", [P, CHUNK])
        causal_sb = sb("causal_sb", [P, CHUNK])
        position_sb = sb("position_sb", [C, CHUNK])
        to_end_sb = sb("to_end_sb", [P, 1])
        same_head_sb = sb("same_head_sb", [C, C])
        decay_mask = sb("decay_mask", [P, HEADS, CHUNK])
        q_decay = sb("q_decay", [C, CHUNK])
        k_decay = sb("k_decay", [P, HEADS])
        chunk_decay = sb("chunk_decay", [C, 1])
        wg_sb = sb("wg_sb", [P, EXPERTS])
        wg_part = sb("wg_part", [P, 2 * EXPERTS], F32R)
        bg_sb = sb("bg_sb", [P, EXPERTS])
        numbers_sb = sb("numbers_sb", [P, EXPERTS])
        w1_sb = sb("w1_sb", [P, EXPERTS * HALVES, P])
        w1_part = [sb(f"w1_part{n}", [P, EXPERTS * HALVES, P], F32R) for n in range(2)]
        b1_sb = sb("b1_sb", [P, EXPERTS * HALVES])
        w2_sb = sb("w2_sb", [P, EXPERTS * HALVES, C])
        b2_sb = sb("b2_sb", [P, PAIRS])
        minus_half = sb("minus_half", [P, TILES])
        eps = sb("eps", [P, TILES])
        warm = sb("warm", [P, 1])

        xin = [sb(f"xin{s}", [P, TILES, CHUNK]) for s in range(2)]
        feat = [[sb(f"feat{s}{n}", [P, GT]) for n in range(2)] for s in range(2)]
        embed_T = sb("embed_T", [P, GT])
        h = [sb(f"h{s}", [P, TILES, C]) for s in range(2)]
        h_plus = [sb(f"h_plus{s}", [P, TILES, C]) for s in range(2)]
        stats = [sb(f"stats{n}", [P, TILES, 6]) for n in range(2)]
        moments = [sb(f"moments{n}", [P, TILES, 2]) for n in range(2)]
        rstd = [sb(f"rstd{n}", [P, TILES]) for n in range(2)]
        normed = [sb(f"normed{n}", [P, TILES, 2, C]) for n in range(2)]
        xs = sb("xs", [P, GT], F32R)
        qk_part = sb("qk_part", [P, 3, GT], BF16)
        qk_rest = sb("qk_rest", [P, GT])
        q_stack = [sb(f"q_stack{s}", [STACK, HEADS, GT], BF16) for s in range(2)]
        k_stack = [sb(f"k_stack{s}", [STACK, HEADS, GT], BF16) for s in range(2)]
        q_dec = [sb(f"q_dec{s}", [C, TILES, CHUNK]) for s in range(2)]
        k_dec = [sb(f"k_dec{s}", [P, TILES, C]) for s in range(2)]
        v = [sb(f"v{s}", [P, TILES, C]) for s in range(2)]
        v_pad = [sb(f"v_pad{s}", [P, TILES, HEADS, 4 * D]) for s in range(2)]

        probs = [sb(f"probs{n}", [P, HEADS, CHUNK]) for n in range(2)]
        heads_T = sb("heads_T", [P, 2, CHUNK])
        state = sb("state", [C, IMAGES, C])
        state_new = sb("state_new", [C, TILES, C])
        h2 = [sb(f"h2{s}", [P, TILES, C]) for s in range(2)]
        xs2 = [sb(f"xs2{s}", [P, GT], F32R) for s in range(2)]

        gate_a = sb("gate_a", [P, TILES, EXPERTS])
        gate = sb("gate", [P, TILES, EXPERTS])
        top = sb("top", [P, TILES, 8])
        top_at = sb("top_at", [P, TILES, 8], U32)
        top_gap = sb("top_gap", [P, TILES])
        top_tanh = sb("top_tanh", [P, TILES])
        top_w = sb("top_w", [P, 2, TILES])
        is_top = [sb(f"is_top{n}", [P, TILES, EXPERTS]) for n in range(2)]
        top_part = [sb(f"top_part{n}", [P, TILES, EXPERTS]) for n in range(2)]
        expert_w = [sb(f"expert_w{s}", [P, TILES, EXPERTS]) for s in range(2)]
        hidden = [sb(f"hidden{n}", [P, GT]) for n in range(4)]
        y_T = [sb(f"y_T{n}", [P, GT]) for n in range(2)]
        weighted = [sb(f"weighted{n}", [P, TILES, 2, C]) for n in range(2)]
        acc = [sb(f"acc{s}", [P, TILES, C]) for s in range(2)]

        def bank(name):
            return ctx.enter_context(nc.psum_tensor(name, [P, 512], F32))

        up_ps = [bank("up_ps0"), bank("up_ps1")]
        down_ps = bank("down_ps")
        token_ps = bank("token_ps")
        score_ps = [bank("score_ps0"), bank("score_ps1")]
        att_ps = bank("att_ps")
        front_ps = bank("front_ps")

        loaded = sem("loaded")
        n_loads = 0
        setup_v = sem("setup_v")
        setup_s = sem("setup_s")
        setup_p = sem("setup_p")
        setup_t = sem("setup_t")
        x_loaded = [sem(f"x_loaded{s}") for s in range(2)]
        stacked = [sem(f"stacked{s}") for s in range(2)]
        stored = [sem(f"stored{s}") for s in range(2)]
        tanh_done = sem("tanh_done")
        tanh_x = sem("tanh_x")
        silu_done = sem("silu_done")
        embed_ready = sem("embed_ready")
        embed_copied = sem("embed_copied")
        embed_turned = sem("embed_turned")
        h_done = sem("h_done")
        stats_done = [sem("stats_done0"), sem("stats_done1")]
        moments_done = [sem("moments_done0"), sem("moments_done1")]
        var_done = [sem("var_done0"), sem("var_done1")]
        rstd_done = [sem("rstd_done0"), sem("rstd_done1")]
        normed_done = [sem("normed_done0"), sem("normed_done1")]
        turned = [sem("turned0"), sem("turned1")]
        xs_high = [sem("xs_high0"), sem("xs_high1")]
        xs_done = [sem("xs_done0"), sem("xs_done1")]
        h_plus_done = sem("h_plus_done")
        qk_ready = sem("qk_ready")
        part_high = sem("part_high")
        rest_done = sem("rest_done")
        q_dec_done = sem("q_dec_done")
        part_mid = sem("part_mid")
        part_low = sem("part_low")
        kv_ready = sem("kv_ready")
        v_done = sem("v_done")
        k_dec_done = sem("k_dec_done")
        v_pad_done = sem("v_pad_done")
        scores_ready = sem("scores_ready")
        probs_done = sem("probs_done")
        heads_ready = sem("heads_ready")
        heads_copied = sem("heads_copied")
        proj_ready = sem("proj_ready")
        h2_done = sem("h2_done")
        outer_ready = sem("outer_ready")
        outer_masked = sem("outer_masked")
        state_done = sem("state_done")
        gate_ready = sem("gate_ready")
        gate_step = sem("gate_step")
        top_tanh_done = sem("top_tanh_done")
        up_ready = sem("up_ready")
        gelu_done = sem("gelu_done")
        down_done = sem("down_done")
        y_copied = sem("y_copied")
        y_turned = sem("y_turned")
        weighted_done = sem("weighted_done")
        acc_done = sem("acc_done")

        GATE = 10
        SETUP_P = 3

        block = ctx.enter_context(nc.Block())

        def values(eng, *counts):
            return [n if isinstance(n, int) else eng.compute_val(n) for n in counts]

        def steps(eng, step):
            for c in range(LEAD):
                step(Turn(None, c))
            with eng.Fori(0, LOOPS) as i:
                for c in range(LEAD, LEAD + 2):
                    step(Turn(i, c))
            for c in range(LEAD + 2 * LOOPS, GROUPS + 3):
                step(Turn(None, c))

        loads = [
            (ident, identity), (front_w_sb, front_w), (front_scale_sb, front_scale), (front_b_sb, front_bias),
            (slope_cols_sb, slope_cols), (slope_rows_sb, slope_rows), (distance_sb, distance),
            (causal_sb, causal), (position_sb, position), (to_end_sb, to_end), (same_head_sb, same_head),
            (wqk_sb, wqk), (wkv_sb, wkv), (wproj_sb, wproj), (bproj_sb, bproj), (wg_sb, wg), (bg_sb, bg),
            (numbers_sb, expert_numbers), (b1_sb, b1), (b2_sb, b2), (w1_sb, w1), (w2_sb, w2),
        ]
        ALL_LOADED = 16 * len(loads)

        @block.sync
        def _(sp):
            def load_x(u):
                if u.back(2).exists:
                    tanhs, silus = values(sp, u.back(2).count(2), u.back(2).count(1))
                    sp.wait_ge(tanh_done, tanhs)
                    sp.wait_ge(silu_done, silus)
                src = x[TILES * u.slot:TILES * (u.slot + 1), :, bass.ds(u.chunk * CHUNK, CHUNK)]
                for half in range(2):
                    sp.dma_start(xin[u.slot][C * half:C * (half + 1), :, :],
                                 src.rearrange("b c t -> c b t")).then_inc(x_loaded[u.slot], 16)

            def stack(u):
                high, mid, low, scored = values(sp, u.count(1), u.count(1), u.count(1), u.back(2).count(8))
                if u.back(2).exists:
                    sp.wait_ge(scores_ready, scored)
                for part, written, count in ((0, part_high, high), (1, part_mid, mid), (2, part_low, low)):
                    sp.wait_ge(written, count)
                    for rows, stacks, parts in ((0, q_stack, Q_PARTS), (C, k_stack, K_PARTS)):
                        for m in range(len(parts)):
                            if parts[m] == part:
                                sp.dma_start(stacks[u.slot][m * D:(m + 1) * D, :, :], qk_part[rows:rows + C, part, :])\
                                    .then_inc(stacked[u.slot], 16)

            def store(w):
                sp.wait_ge(acc_done, w.count(8))
                dst = out[TILES * w.slot:TILES * (w.slot + 1), bass.ds(w.chunk * CHUNK, CHUNK), :]
                sp.dma_start(dst.rearrange("b t c -> t b c"), acc[w.slot][:, :, :]).then_inc(stored[w.slot], 16)

            def step(u):
                if u.ahead(2).exists:
                    load_x(u.ahead(2))
                if u.back(3).exists:
                    store(u.back(3))
                if u.exists:
                    stack(u)

            load_x(Turn(None, 0))
            for dst, src in loads:
                sp.dma_start(dst[:], src).then_inc(loaded, 16)
            load_x(Turn(None, 1))
            steps(sp, step)
            for s in range(2):
                sp.wait_ge(stored[s], 16 * GROUPS // 2)

        @block.gpsimd
        def _(pool):
            gp = nc.gpsimd
            gp.memset(minus_half[:], -0.5)
            gp.memset(eps[:], EPS)
            gp.memset(spline_rows[:], 1.0).then_inc(setup_p, 1)
            pool.wait_ge(setup_p, 1)
            gp.memset(spline_rows[0:C, 0:1], 0.0).then_inc(setup_p, 1)
            pool.wait_ge(setup_p, 2)
            gp.memset(state[:], 0.0)
            for s in range(2):
                gp.memset(v_pad[s][:], 0.0)
            gp.memset(warm[:], 0.0).then_inc(setup_p, 1)
            pool.wait_ge(setup_p, SETUP_P)

            def silu(u):
                f, x_rows = feat[u.slot][0][0:C, :], xin[u.slot][0:C, :, :].rearrange("c b t -> c (b t)")
                pool.wait_ge(tanh_done, u.count(2))
                gp.tensor_tensor(f, f, x_rows, ALU.mult).then_inc(tanh_x, 1)
                pool.wait_ge(tanh_x, u.count(1))
                gp.tensor_tensor(f, f, x_rows, ALU.add).then_inc(silu_done, 1)

            def rsqrt(n, u):
                pool.wait_ge(moments_done[n], u.count(1))
                if u.back(1).exists:
                    pool.wait_ge(normed_done[n], u.back(1).count(1))
                gp.tensor_tensor(rstd[n][:, :], moments[n][:, :, 1], eps[:, :], ALU.add)\
                    .then_inc(var_done[n], 1)
                pool.wait_ge(var_done[n], u.count(1))
                gp.tensor_tensor(rstd[n][:, :], rstd[n][:, :], minus_half[:, :], ALU.pow)\
                    .then_inc(rstd_done[n], 1)

            def residual(u):
                pool.wait_ge(h_done, u.count(1))
                if u.back(2).exists:
                    pool.wait_ge(h2_done, u.back(2).count(1))
                gp.tensor_tensor(h_plus[u.slot][:, :, :], h[u.slot][:, :, :],
                                 bproj_sb[:, :].unsqueeze(1).to_broadcast([P, TILES, C]), ALU.add)\
                    .then_inc(h_plus_done, 1)

            def low_parts(u):
                pool.wait_ge(part_mid, u.count(1))
                gp.tensor_tensor(qk_part[:, 2, :], qk_rest[:, :], qk_part[:, 1, :], ALU.subtract)\
                    .then_inc(part_low, 1)

            def pad_v(u):
                copied, used = values(pool, u.count(1), u.back(2).count(4))
                pool.wait_ge(loaded, ALL_LOADED)
                pool.wait_ge(v_done, copied)
                if u.back(2).exists:
                    pool.wait_ge(heads_ready, used)
                for b in range(TILES):
                    for a in range(2):
                        dst = v_pad[u.slot][:, b, 4 * a:4 * a + 4, :].rearrange("p r k -> p (r k)")
                        last = gp.tensor_copy(
                            bass.AP(dst.tensor, dst.offset, [list(dst.ap[0]), [5 * D, 4], [1, D]]),
                            v[u.slot][:, b, 4 * D * a:4 * D * (a + 1)].rearrange("p (r k) -> p r k", r=4))
                    last.then_inc(v_pad_done, 1)

            def add_experts(w, p):
                pool.wait_ge(weighted_done, w.count(4, p + 1))
                for e in range(2):
                    n = 2 * p + e
                    if n == 0:
                        if w.back(2).exists:
                            pool.wait_ge(stored[w.slot], w.back(2).slot_count(16))
                        before = h2[w.slot][:, :, :]
                    else:
                        pool.wait_ge(acc_done, w.count(8, n))
                        before = acc[w.slot][:, :, :]
                    gp.tensor_tensor(acc[w.slot][:, :, :], before, weighted[p % 2][:, :, e, :], ALU.add)\
                        .then_inc(acc_done, 1)

            pool.wait_ge(loaded, ALL_LOADED)

            silu(Turn(None, 0))

            def step(u):
                att, ffn, old, new = u.back(1), u.back(2), u.back(3), u.ahead(1)
                if att.exists:
                    pad_v(att)
                if old.exists:
                    add_experts(old, 2)
                    add_experts(old, 3)
                if u.exists:
                    rsqrt(0, u)
                    residual(u)
                if ffn.exists:
                    add_experts(ffn, 0)
                if u.exists:
                    low_parts(u)
                if att.exists:
                    rsqrt(1, att)
                if ffn.exists:
                    add_experts(ffn, 1)
                if new.exists:
                    silu(new)

            steps(pool, step)

        @block.scalar
        def _(act):
            sc = nc.scalar
            act.wait_ge(setup_v, 1)
            for hd in range(HEADS):
                sc.activation(decay_mask[:, hd, :], distance_sb[:, :], ACT.Exp, scale=slope_rows_sb[:, hd:hd + 1])
            sc.activation(q_decay[:, :], position_sb[:, :], ACT.Exp, scale=slope_cols_sb[:, 0:1])
            sc.activation(k_decay[:, :], slope_rows_sb[:, :], ACT.Exp, scale=to_end_sb[:, 0:1])
            sc.activation(chunk_decay[:, :], slope_cols_sb[:, :], ACT.Exp, scale=float(CHUNK)).then_inc(setup_s, 1)
            act.wait_ge(setup_p, SETUP_P)
            act.wait_ge(setup_s, 1)
            sc.activation(warm[:, :], warm[:, :], ACT.Gelu).then_inc(setup_s, 1)
            act.wait_ge(setup_v, 5)

            def tanhs(u):
                act.wait_ge(x_loaded[u.slot], u.slot_count(32))
                if u.back(2).exists:
                    act.wait_ge(embed_ready, u.back(2).count(1))
                for n in range(2):
                    sc.activation(feat[u.slot][n][:, :], xin[u.slot][:, :, :].rearrange("c b t -> c (b t)"),
                                  ACT.Tanh, scale=front_scale_sb[:, n:n + 1]).then_inc(tanh_done, 1)

            def copy_embed(u):
                act.wait_ge(embed_ready, u.count(1))
                if u.back(1).exists:
                    act.wait_ge(embed_turned, u.back(1).count(1))
                sc.activation(embed_T[:, :], front_ps[:, :], ACT.Identity, bias=embed_bias[:, 0:1])\
                    .then_inc(embed_copied, 1)

            def high_xs(n, u):
                act.wait_ge(turned[n], u.count(1))
                if n == 0:
                    if u.back(1).exists:
                        act.wait_ge(kv_ready, u.back(1).count(1))
                    sc.activation(xs[:, :], front_ps[:, :], ACT.Copy).then_inc(xs_high[0], 1)
                else:
                    if u.back(2).exists:
                        act.wait_ge(gate_ready, u.back(2).count(1))
                        act.wait_ge(up_ready, u.back(2).count(16))
                    sc.activation(xs2[u.slot][:, :], att_ps[:, :], ACT.Copy).then_inc(xs_high[1], 1)

            def high_parts(u):
                act.wait_ge(qk_ready, u.count(1))
                if u.back(1).exists:
                    act.wait_ge(stacked[u.back(1).slot], u.back(1).slot_count(12 * 16))
                sc.activation(qk_part[:, 0, :], front_ps[:, :], ACT.Copy).then_inc(part_high, 1)

            def mid_parts(u):
                act.wait_ge(rest_done, u.count(1))
                sc.activation(qk_part[:, 1, :], qk_rest[:, :], ACT.Copy).then_inc(part_mid, 1)

            def copy_v(u):
                act.wait_ge(kv_ready, u.count(1))
                if u.back(2).exists:
                    act.wait_ge(outer_ready, u.back(2).count(1))
                    act.wait_ge(v_pad_done, u.back(2).count(4))
                kv = front_ps[:, :].rearrange("p (b k) -> p b k", b=TILES)
                sc.activation(v[u.slot][:, :, :], kv[:, :, C:2 * C], ACT.Copy).then_inc(v_done, 1)

            def copy_heads(a):
                act.wait_ge(heads_ready, a.count(4))
                if a.back(1).exists:
                    act.wait_ge(proj_ready, a.back(1).count(1))
                sc.activation(heads_T[:, :, :].rearrange("p a t -> p (a t)"), att_ps[:, 0:2 * CHUNK], ACT.Copy)\
                    .then_inc(heads_copied, 1)

            def gate_tanh(w):
                act.wait_ge(gate_step, w.count(GATE, 4))
                sc.activation(top_tanh[:, :], top_gap[:, :], ACT.Tanh, scale=0.5).then_inc(top_tanh_done, 1)

            def gelus(w, j):
                for k in range(2):
                    n = 2 * j + k
                    act.wait_ge(up_ready, w.count(16, n + 1))
                    if j >= 2 or w.back(1).exists:
                        act.wait_ge(down_done, w.count(8, j - 1))
                    chunk = chunk_of(n)
                    sc.activation(hidden[n % 4][:, :], up_ps[n % 2][:, :], ACT.Gelu, bias=b1_sb[:, chunk:chunk + 1])\
                        .then_inc(gelu_done, 1)

            def copy_y(w, p):
                act.wait_ge(down_done, w.count(8, 2 * p + 2))
                if p >= 2 or w.back(1).exists:
                    act.wait_ge(y_turned, w.count(4, p - 1))
                sc.activation(y_T[p % 2][:, :], down_ps[:, :], ACT.Identity, bias=b2_sb[:, p:p + 1])\
                    .then_inc(y_copied, 1)

            tanhs(Turn(None, 0))

            def step(u):
                a, w, new = u.back(1), u.back(2), u.ahead(1)
                for j in range(8):
                    if j == 1 and u.exists:
                        copy_embed(u)
                    if w.exists:
                        gelus(w, j)
                        if j in (2, 4, 6):
                            copy_y(w, j // 2 - 1)
                    if j == 3 and u.exists:
                        high_xs(0, u)
                    if j == 3 and w.exists:
                        gate_tanh(w)
                    if j == 4 and u.exists:
                        high_parts(u)
                    if j == 4 and a.exists:
                        copy_heads(a)
                    if j == 5 and u.exists:
                        mid_parts(u)
                    if j == 7 and new.exists:
                        tanhs(new)
                if a.exists:
                    high_xs(1, a)
                if w.exists:
                    copy_y(w, 3)
                if u.exists:
                    copy_v(u)

            steps(act, step)

        @block.vector
        def _(dve):
            ve = nc.vector

            def bc(ap, n, k):
                return ap.unsqueeze(1).to_broadcast([ap.shape[0], n, k])

            dve.wait_ge(loaded, ALL_LOADED)
            ve.tensor_scalar(slope_cols_sb[:, :], slope_cols_sb[:, :], -1.0, None, ALU.mult)
            ve.tensor_scalar(slope_rows_sb[:, :], slope_rows_sb[:, :], -1.0, None, ALU.mult).then_inc(setup_v, 1)
            ve.tensor_scalar(front_scale_sb[:, :], front_scale_sb[:, :], 0.5, None, ALU.mult)
            ve.tensor_scalar(front_w_sb[:, :, :], front_w_sb[:, :, :], 0.5, None, ALU.mult)
            ve.tensor_copy(wg_part[:, 0:EXPERTS], wg_sb[:, :]).then_inc(setup_v, 1)
            for part, whole in ((wqk_part, wqk_sb), (wkv_part, wkv_sb), (w1_part, w1_sb)):
                last = ve.tensor_copy(part[0][:], whole[:])
            last.then_inc(setup_v, 1)
            dve.wait_ge(setup_v, 3)
            ve.tensor_tensor(wg_part[:, EXPERTS:2 * EXPERTS], wg_sb[:, :], wg_part[:, 0:EXPERTS].bitcast(F32),
                             ALU.subtract)
            for part, whole in ((wqk_part, wqk_sb), (wkv_part, wkv_sb), (w1_part, w1_sb)):
                ve.tensor_tensor(part[1][:], whole[:], part[0][:].bitcast(F32), ALU.subtract)
            dve.wait_ge(setup_s, 1)
            ve.tensor_scalar(q_decay[:, :], q_decay[:, :], SCALE, None, ALU.mult)
            ve.tensor_tensor(decay_mask[:, :, :], decay_mask[:, :, :], bc(causal_sb[:, :], HEADS, CHUNK),
                             ALU.mult).then_inc(setup_v, 1)
            dve.wait_ge(setup_v, 4)
            dve.wait_ge(setup_t, 1)
            ve.tensor_tensor(embed_bias[:, :], front_b_sb[:, :], front_ps[:, 0:1], ALU.add).then_inc(setup_v, 1)

            def layer_norm_moments(n, u, src):
                for b in range(TILES):
                    last = ve.bn_stats(stats[n][:, b, :], src[:, b, :])
                last.then_inc(stats_done[n], 1)
                summed, = values(dve, u.count(1))
                dve.wait_ge(loaded, ALL_LOADED)
                dve.wait_ge(stats_done[n], summed)
                for b in range(TILES):
                    last = ve.bn_aggr(moments[n][:, b, :], stats[n][:, b, :])
                last.then_inc(moments_done[n], 1)

            def layer_norm(n, u, src):
                dve.wait_ge(rstd_done[n], u.count(1))
                if u.back(1).exists:
                    dve.wait_ge(turned[n], u.back(1).count(1))
                for b in range(TILES):
                    last = ve.tensor_scalar(normed[n][:, b, :, :], bc(src[:, b, :], 2, C),
                                            moments[n][:, b, 0:1], rstd[n][:, b:b + 1], ALU.subtract, ALU.mult)
                last.then_inc(normed_done[n], 1)

            def embed(u):
                dve.wait_ge(embed_turned, u.count(1))
                ve.tensor_reduce(h[u.slot][:, :, :], front_ps[:, :].rearrange("p (b n c) -> p b c n", b=TILES, n=2),
                                 mybir.AxisListType.X, ALU.add).then_inc(h_done, 1)
                dve.wait_ge(h_done, u.count(1))
                layer_norm_moments(0, u, h[u.slot])

            def low_xs(n, u):
                dve.wait_ge(xs_high[n], u.count(1))
                to, ps = (xs, front_ps) if n == 0 else (xs2[u.slot], att_ps)
                ve.tensor_tensor(to[C:P, :], ps[C:P, :], to[C:P, :].bitcast(F32), ALU.subtract)\
                    .then_inc(xs_done[n], 1)

            def split_qk(u):
                dve.wait_ge(part_high, u.count(1))
                if u.back(1).exists:
                    dve.wait_ge(part_low, u.back(1).count(1))
                ve.tensor_tensor(qk_rest[:, :], front_ps[:, :], qk_part[:, 0, :], ALU.subtract).then_inc(rest_done, 1)
                if u.back(2).exists:
                    dve.wait_ge(heads_ready, u.back(2).count(4))
                ve.tensor_tensor(q_dec[u.slot][:, :, :], front_ps[0:C, :].rearrange("p (b t) -> p b t", b=TILES),
                                 bc(q_decay[:, :], TILES, CHUNK), ALU.mult).then_inc(q_dec_done, 1)

            def decay_k(u):
                dve.wait_ge(v_done, u.count(1))
                if u.back(2).exists:
                    dve.wait_ge(outer_ready, u.back(2).count(1))
                kv = front_ps[:, :].rearrange("p (b k) -> p b k", b=TILES)
                for b in range(TILES):
                    last = ve.tensor_tensor(k_dec[u.slot][:, b, :].rearrange("p (d h) -> p d h", h=HEADS),
                                            kv[:, b, 0:C].rearrange("p (d h) -> p d h", h=HEADS),
                                            bc(k_decay[:, :], D, HEADS), ALU.mult)
                last.then_inc(k_dec_done, 1)

            def mask_scores(a, b):
                for half in range(2):
                    dve.wait_ge(scores_ready, a.count(8, 2 * b + half + 1))
                    if b >= 2 or a.back(1).exists:
                        dve.wait_ge(heads_ready, a.count(4, b - 1))
                    ve.tensor_tensor(probs[b % 2][:, 4 * half:4 * half + 4, :],
                                     score_ps[half][:, :].rearrange("p (h t) -> p h t", h=4),
                                     decay_mask[:, 4 * half:4 * half + 4, :], ALU.mult).then_inc(probs_done, 1)

            def add_attention(a):
                dve.wait_ge(proj_ready, a.count(1))
                dve.wait_ge(h_plus_done, a.count(1))
                if a.back(2).exists:
                    dve.wait_ge(acc_done, a.back(2).count(8, 1))
                ve.tensor_tensor(h2[a.slot][:, :, :], att_ps[:, 0:TILES * C].rearrange("p (b c) -> p b c", b=TILES),
                                 h_plus[a.slot][:, :, :], ALU.add).then_inc(h2_done, 1)
                dve.wait_ge(h2_done, a.count(1))
                layer_norm_moments(1, a, h2[a.slot])

            def carry_state(a):
                dve.wait_ge(outer_ready, a.count(1))
                ve.tensor_tensor(state_new[:, :, :], front_ps[0:C, 0:TILES * C].rearrange("p (b c) -> p b c", b=TILES),
                                 bc(same_head_sb[:, :], TILES, C), ALU.mult).then_inc(outer_masked, 1)
                dve.wait_ge(outer_masked, a.count(1))
                dve.wait_ge(heads_ready, a.count(4))
                own = state[:, TILES * a.slot:TILES * (a.slot + 1), :]
                ve.scalar_tensor_tensor(own, own, chunk_decay[:, 0:1], state_new[:, :, :], ALU.mult, ALU.add)\
                    .then_inc(state_done, 1)

            def top_two(w):
                dve.wait_ge(gate_ready, w.count(1))
                both = token_ps[:, 0:TILES * 2 * EXPERTS].rearrange("p (b k) -> p b k", b=TILES)
                ve.tensor_tensor(gate_a[:, :, :], both[:, :, 0:EXPERTS], bc(bg_sb[:, :], TILES, EXPERTS), ALU.add)\
                    .then_inc(gate_step, 1)
                dve.wait_ge(gate_step, w.count(GATE, 1))
                ve.tensor_tensor(gate[:, :, :], gate_a[:, :, :], both[:, :, EXPERTS:2 * EXPERTS], ALU.add)\
                    .then_inc(gate_step, 1)
                summed, = values(dve, w.count(GATE, 2))
                dve.wait_ge(loaded, ALL_LOADED)
                dve.wait_ge(gate_step, summed)
                for b in range(TILES):
                    last = ve.max(top[:, b, :], gate[:, b, :])
                last.then_inc(gate_step, 1)
                dve.wait_ge(gate_step, w.count(GATE, 3))
                ve.tensor_tensor(top_gap[:, :], top[:, :, 0], top[:, :, 1], ALU.subtract).then_inc(gate_step, 1)
                for b in range(TILES):
                    last = ve.max_index(top_at[:, b, :], top[:, b, :], gate[:, b, :])
                last.then_inc(gate_step, 1)

            def weigh_top(w):
                dve.wait_ge(gate_step, w.count(GATE, 5))
                dve.wait_ge(top_tanh_done, w.count(1))
                for n in range(2):
                    ve.tensor_scalar(top_w[:, n, :], top_tanh[:, :], 0.5 - n, 0.5, ALU.mult, ALU.add)
                    last = ve.tensor_tensor(is_top[n][:, :, :], bc(numbers_sb[:, :], TILES, EXPERTS),
                                            top_at[:, :, n:n + 1].to_broadcast([P, TILES, EXPERTS]), ALU.is_equal)
                    last.then_inc(gate_step, 1)
                dve.wait_ge(gate_step, w.count(GATE, 7))
                for n in range(2):
                    ve.tensor_tensor(top_part[n][:, :, :], is_top[n][:, :, :],
                                     top_w[:, n, :].unsqueeze(2).to_broadcast([P, TILES, EXPERTS]), ALU.mult)\
                        .then_inc(gate_step, 1)
                dve.wait_ge(gate_step, w.count(GATE, 9))
                ve.tensor_tensor(expert_w[w.slot][:, :, :], top_part[0][:, :, :], top_part[1][:, :, :], ALU.add)\
                    .then_inc(gate_step, 1)

            def weigh(w, p):
                dve.wait_ge(y_turned, w.count(4, p + 1))
                if p == 0:
                    dve.wait_ge(gate_step, w.count(GATE))
                if p >= 2 or w.back(1).exists:
                    dve.wait_ge(acc_done, w.count(8, 2 * p - 2))
                ve.tensor_tensor(weighted[p % 2][:, :, :, :],
                                 token_ps[:, :].rearrange("p (b e c) -> p b e c", b=TILES, e=2),
                                 expert_w[w.slot][:, :, 2 * p:2 * p + 2].unsqueeze(3).to_broadcast([P, TILES, 2, C]),
                                 ALU.mult).then_inc(weighted_done, 1)

            def step(u):
                a, w, old = u.back(1), u.back(2), u.back(3)
                for j in range(9):
                    if j < 4 and a.exists:
                        mask_scores(a, j)
                    if j == 0 and old.exists:
                        weigh(old, 3)
                    if j == 1 and u.exists:
                        embed(u)
                    if j == 2 and w.exists:
                        top_two(w)
                    if j == 2 and u.exists:
                        layer_norm(0, u, h[u.slot])
                    if j == 3 and u.exists:
                        low_xs(0, u)
                    if j == 3 and w.exists:
                        weigh_top(w)
                    if j == 4 and w.exists:
                        weigh(w, 0)
                    if j == 4 and u.exists:
                        split_qk(u)
                    if j == 5 and w.exists:
                        weigh(w, 1)
                    if j == 5 and a.exists:
                        add_attention(a)
                    if j == 6 and a.exists:
                        layer_norm(1, a, h2[a.slot])
                    if j == 6 and a.exists:
                        carry_state(a)
                    if j == 8 and a.exists:
                        low_xs(1, a)
                    if j == 8 and w.exists:
                        weigh(w, 2)
                    if j == 8 and u.exists:
                        decay_k(u)

            steps(dve, step)

        @block.tensor
        def _(pe):
            te = nc.tensor
            pe.wait_ge(loaded, ALL_LOADED)
            pe.wait_ge(setup_p, SETUP_P)
            pe.wait_ge(setup_v, 4)
            for n in range(2):
                last = te.matmul(front_ps[C * n:C * (n + 1), 0:1], front_w_sb[:, n, :], spline_rows[:, n:n + 1],
                                 start=True, stop=True)
            last.then_inc(setup_t, 1)
            pe.wait_ge(setup_v, 5)

            def up(w, j):
                for k in range(2):
                    n = 2 * j + k
                    if n == 0:
                        pe.wait_ge(xs_done[1], w.count(1))
                    if n >= 2 or w.back(1).exists:
                        pe.wait_ge(gelu_done, w.count(16, n - 1))
                    chunk = chunk_of(n)
                    te.matmul(up_ps[n % 2][:, :], w1_part[0][:, chunk, :], xs2[w.slot][:, :], start=True, stop=False)
                    te.matmul(up_ps[n % 2][:, :], w1_part[1][:, chunk, :], xs2[w.slot][:, :], start=False, stop=True)\
                        .then_inc(up_ready, 1)

            def down(w, j):
                pe.wait_ge(gelu_done, w.count(16, 2 * j + 2))
                if j % 2 == 0 and (j or w.back(1).exists):
                    pe.wait_ge(y_copied, w.count(4, j // 2))
                for k in range(2):
                    n = 2 * j + k
                    last = te.matmul(down_ps[C * k:C * (k + 1), :], w2_sb[:, chunk_of(n), :], hidden[n % 4][:, :],
                                     start=j % 2 == 0, stop=j % 2 == 1)
                last.then_inc(down_done, 1)

            def turn_y(w, p):
                pe.wait_ge(y_copied, w.count(4, p + 1))
                if p == 0:
                    pe.wait_ge(gate_step, w.count(GATE, 2))
                else:
                    pe.wait_ge(weighted_done, w.count(4, p))
                for b in range(TILES):
                    last = te.transpose(token_ps[:, P * b:P * (b + 1)], y_T[p % 2][:, CHUNK * b:CHUNK * (b + 1)],
                                        ident[:, :])
                last.then_inc(y_turned, 1)

            def gate_logits(w):
                if w.back(1).exists:
                    pe.wait_ge(weighted_done, w.back(1).count(4))
                for b in range(TILES):
                    last = te.matmul(token_ps[:, 2 * EXPERTS * b:2 * EXPERTS * (b + 1)],
                                     xs2[w.slot][:, CHUNK * b:CHUNK * (b + 1)], wg_part[:, :], start=True, stop=True)
                last.then_inc(gate_ready, 1)

            def scores(a, b):
                if b == 0:
                    pe.wait_ge(stacked[a.slot], a.slot_count(12 * 16))
                for half in range(2):
                    if b or a.back(1).exists:
                        pe.wait_ge(probs_done, a.count(8, 2 * b + half - 1))
                    for r in range(4):
                        hd = 4 * half + r
                        cols = slice(CHUNK * b, CHUNK * (b + 1))
                        last = te.matmul(score_ps[half][:, CHUNK * r:CHUNK * (r + 1)], k_stack[a.slot][:, hd, cols],
                                         q_stack[a.slot][:, hd, cols], start=True, stop=True)
                    last.then_inc(scores_ready, 1)

            def heads(a, b):
                if b == 0:
                    pe.wait_ge(q_dec_done, a.count(1))
                    if a.back(1).exists:
                        pe.wait_ge(xs_done[1], a.back(1).count(1))
                    if a.back(2).exists:
                        pe.wait_ge(state_done, a.back(2).count(1))
                padded, masked = values(pe, a.count(4, b + 1), a.count(8, 2 * b + 2))
                pe.wait_ge(loaded, ALL_LOADED)
                pe.wait_ge(v_pad_done, padded)
                pe.wait_ge(probs_done, masked)
                top_row, cols = C * (b % 2), slice(CHUNK * (b // 2), CHUNK * (b // 2 + 1))
                te.matmul(att_ps[top_row:top_row + C, cols], state[:, TILES * a.slot + b, :], q_dec[a.slot][:, b, :],
                          start=True, stop=False, skip_group_check=True)
                for r in range(4):
                    for half in range(2):
                        row = top_row + 32 * half
                        last = te.matmul(att_ps[row:row + 32, cols], v_pad[a.slot][:, b, 4 * half + r, :],
                                         probs[b % 2][:, 4 * half + r, :], start=False, stop=r == 3,
                                         skip_group_check=True)
                last.then_inc(heads_ready, 1)

            def project(a):
                pe.wait_ge(heads_copied, a.count(1))
                for pair in range(2):
                    last = te.matmul(att_ps[:, P * pair:P * (pair + 1)], heads_T[:, pair, :], wproj_sb[:, :],
                                     start=True, stop=True)
                last.then_inc(proj_ready, 1)

            def turn(n, u):
                pe.wait_ge(normed_done[n], u.count(1))
                ps = front_ps if n == 0 else att_ps
                for b in range(TILES):
                    last = te.transpose(ps[:, CHUNK * b:CHUNK * (b + 1)],
                                        normed[n][:, b, :, :].rearrange("p r c -> p (r c)"), ident[:, :])
                last.then_inc(turned[n], 1)

            def embedding(u):
                pe.wait_ge(tanh_done, u.count(2))
                pe.wait_ge(silu_done, u.count(1))
                if u.back(1).exists:
                    pe.wait_ge(k_dec_done, u.back(1).count(1))
                for n in range(2):
                    last = te.matmul(front_ps[C * n:C * (n + 1), :], front_w_sb[:, n, :], feat[u.slot][n][:, :],
                                     start=True, stop=True)
                last.then_inc(embed_ready, 1)

            def turn_embed(u):
                pe.wait_ge(embed_copied, u.count(1))
                for b in range(TILES):
                    last = te.transpose(front_ps[:, P * b:P * (b + 1)], embed_T[:, CHUNK * b:CHUNK * (b + 1)],
                                        ident[:, :])
                last.then_inc(embed_turned, 1)

            def project_qk(u):
                pe.wait_ge(xs_done[0], u.count(1))
                for n in range(2):
                    last = te.matmul(front_ps[:, :], wqk_part[n][:, :], xs[:, :], start=n == 0, stop=n == 1)
                last.then_inc(qk_ready, 1)

            def project_kv(u):
                if u.back(1).exists:
                    pe.wait_ge(outer_masked, u.back(1).count(1))
                else:
                    pe.wait_ge(part_high, u.count(1))
                    pe.wait_ge(q_dec_done, u.count(1))
                for b in range(TILES):
                    for n in range(2):
                        last = te.matmul(front_ps[:, P * b:P * (b + 1)], xs[:, CHUNK * b:CHUNK * (b + 1)],
                                         wkv_part[n][:, :], start=n == 0, stop=n == 1)
                last.then_inc(kv_ready, 1)

            def outer(a, u):
                pe.wait_ge(k_dec_done, a.count(1))
                if u.exists:
                    pe.wait_ge(part_high, u.count(1))
                    pe.wait_ge(q_dec_done, u.count(1))
                for b in range(TILES):
                    last = te.matmul(front_ps[0:C, C * b:C * (b + 1)], k_dec[a.slot][:, b, :], v[a.slot][:, b, :],
                                     start=True, stop=True)
                last.then_inc(outer_ready, 1)

            def step(u):
                a, w, old = u.back(1), u.back(2), u.back(3)
                for j in range(9):
                    if j == 8 and a.exists:
                        turn(1, a)
                    if w.exists:
                        if j < 8:
                            up(w, j)
                        if j >= 1:
                            down(w, j - 1)
                    if j == 0 and old.exists:
                        turn_y(old, 3)
                    if 1 <= j <= 4 and a.exists:
                        heads(a, j - 1)
                    if j <= 3 and a.exists:
                        scores(a, j)
                    if j == 0 and u.exists:
                        embedding(u)
                    if j == 1 and u.exists:
                        turn_embed(u)
                    if j == 1 and w.exists:
                        gate_logits(w)
                    if j == 3 and u.exists:
                        turn(0, u)
                    if j == 4 and w.exists:
                        turn_y(w, 0)
                    if j == 4 and u.exists:
                        project_qk(u)
                    if j == 5 and w.exists:
                        turn_y(w, 1)
                    if j == 5 and a.exists:
                        project(a)
                    if j == 6 and a.exists:
                        outer(a, u)
                    if j == 8 and w.exists:
                        turn_y(w, 2)
                    if j == 8 and u.exists:
                        project_kv(u)

            steps(pe, step)


def chunk_of(n):
    pair, half, e = n // 4, n % 4 // 2, n % 2
    return (2 * pair + e) * HALVES + half


def kernel(**inputs):
    import numpy as np
    import concourse.bacc as bacc
    from concourse.bass_utils import run_bass_kernel_spmd

    f = {k: np.ascontiguousarray(a) for k, a in inputs.items()}
    twice = lambda a: np.concatenate([a, a], axis=0)
    on_diagonal = lambda a: np.block([[a, np.zeros_like(a)], [np.zeros_like(a), a]])
    rows = lambda a, n=P: np.broadcast_to(a, (n,) + a.shape)
    bases, spline = f["L0_tok_bases"], f["L0_tok_W_spline"].reshape(C, C, 3)
    ones = np.ones((C,), np.float32)
    at = np.arange(CHUNK)
    diff = at[None, :] - at[:, None]
    wq, wk, wv = (f["L0_attn_w_qkv"][:, C * n:C * (n + 1)] for n in range(3))
    wq, wk = (a.reshape(C, HEADS, D).transpose(0, 2, 1).reshape(C, C) for a in (wq, wk))
    host = {
        "x": f["x"].reshape(IMAGES, C, TOKENS),
        "front_w": np.stack([np.concatenate([f["L0_tok_W_base"].T, spline[:, :, 0].T]),
                             np.concatenate([spline[:, :, 1].T, spline[:, :, 2].T])], axis=1),
        "front_scale": np.stack([np.concatenate([ones, bases[:, 0]]),
                                 np.concatenate([bases[:, 1], bases[:, 2]])], axis=1),
        "front_bias": np.concatenate([f["L0_tok_b_base"], f["L0_tok_b_spline"]])[:, None],
        "wqk": twice(np.concatenate([wq, wk], axis=1)),
        "wkv": twice(np.concatenate([wk, wv], axis=1)),
        "wproj": on_diagonal(f["L0_attn_w_proj"]),
        "bproj": rows(f["L0_attn_b_proj"]),
        "slope_cols": np.tile(f["L0_attn_slopes"], D)[:, None],
        "slope_rows": rows(f["L0_attn_slopes"]),
        "wg": twice(f["L0_ffn_Wg"]),
        "bg": rows(f["L0_ffn_bg"]),
        "w1": twice(f["L0_ffn_W1"].transpose(1, 0, 2).reshape(C, EXPERTS * HALVES, P)),
        "b1": f["L0_ffn_b1"].reshape(EXPERTS * HALVES, P).T,
        "w2": f["L0_ffn_W2"].reshape(EXPERTS * HALVES, P, C).transpose(1, 0, 2),
        "b2": f["L0_ffn_b2"].reshape(PAIRS, 2 * C).T,
        "identity": np.eye(P, dtype=np.float32),
        "distance": np.maximum(diff, 0).astype(np.float32),
        "causal": np.where(diff >= 0, SCALE, 0.0).astype(np.float32),
        "position": rows(at.astype(np.float32), C),
        "to_end": (CHUNK - at).astype(np.float32)[:, None],
        "same_head": np.kron(np.tile(np.eye(HEADS), (D, 1)), np.ones((1, D))).astype(np.float32),
        "expert_numbers": rows(np.arange(EXPERTS, dtype=np.float32)),
    }
    host = {k: np.ascontiguousarray(a) for k, a in host.items()}
    nc = bacc.Bacc("TRN2", target_bir_lowering=False, num_devices=1)
    args = {k: nc.dram_tensor(f"in_{k}", a.shape, mybir.dt.from_np(a.dtype), kind="ExternalInput").ap()
            for k, a in host.items()}
    out = nc.dram_tensor("out", (IMAGES, TOKENS, C), F32, kind="ExternalOutput").ap()
    build_tower(nc, **args, out=out)
    r = run_bass_kernel_spmd(nc, [{f"in_{k}": a for k, a in host.items()}], core_ids=[0])
    return r.results[0]["out"]
```

```python
import math
from contextlib import ExitStack

import concourse.bass as bass
from concourse import mybir

F32 = mybir.dt.float32
F32R = mybir.dt.float32r
BF16 = mybir.dt.bfloat16
U32 = mybir.dt.uint32
ALU = mybir.AluOpType
ACT = mybir.ActivationFunctionType

P = 128
IMAGES = 8
TOKENS = 4096
CHUNK = 128
CHUNKS = TOKENS // CHUNK
C = 64
HEADS = 8
D = C // HEADS
EXPERTS = 8
HIDDEN = 256
TILES = 4
GT = TILES * CHUNK
GROUPS = IMAGES * TOKENS // GT
PAIRS = EXPERTS // 2
HALVES = HIDDEN // P
SCALE = float(D) ** -0.5
EPS = 1e-5
Q_PARTS = (0, 0, 1, 0, 2, 1)
K_PARTS = (0, 1, 0, 2, 0, 1)
STACK = len(Q_PARTS) * D

LEAD = 4
LOOPS = (GROUPS - LEAD) // 2 - 1


class Turn:

    def __init__(self, i, c):
        self.i, self.c = i, c

    def back(self, n):
        return Turn(self.i, self.c - n)

    def ahead(self, n):
        return Turn(self.i, self.c + n)

    @property
    def exists(self):
        assert self.i is None or self.c >= 0, "peel more steps before the loop"
        return 0 <= self.c and (self.i is not None or self.c < GROUPS)

    @property
    def slot(self):
        return self.c % 2

    @property
    def chunk(self):
        return self.c // 2 if self.i is None else self.i + self.c // 2

    def count(self, per_group, events=None):
        events = per_group if events is None else events
        if self.i is None:
            return per_group * self.c + events
        return self.i * (2 * per_group) + (per_group * self.c + events)

    def slot_count(self, per_group):
        if self.i is None:
            return per_group * (self.c // 2 + 1)
        return self.i * per_group + per_group * (self.c // 2 + 1)


def build_tower(nc, x, front_w, front_scale, front_bias, wqk, wkv, wproj, bproj, slope_cols, slope_rows,
                wg, bg, w1, b1, w2, b2, identity, distance, causal, position, to_end, same_head,
                expert_numbers, out):
    with ExitStack() as ctx:
        def sb(name, shape, dt=F32):
            return ctx.enter_context(nc.sbuf_tensor(name, shape, dt))

        def sem(name):
            return ctx.enter_context(nc.semaphore(name))

        ident = sb("ident", [P, P])
        front_w_sb = sb("front_w_sb", [P, 2, C])
        front_scale_sb = sb("front_scale_sb", [P, 2])
        front_b_sb = sb("front_b_sb", [P, 1])
        embed_bias = sb("embed_bias", [P, 1])
        spline_rows = sb("spline_rows", [P, 2])
        wqk_sb = sb("wqk_sb", [P, P])
        wkv_sb = sb("wkv_sb", [P, P])
        wqk_part = [sb(f"wqk_part{n}", [P, P], F32R) for n in range(2)]
        wkv_parts = sb("wkv_parts", [P, 2, P], F32R)
        wproj_sb = sb("wproj_sb", [P, P])
        bproj_sb = sb("bproj_sb", [P, C])
        slope_cols_sb = sb("slope_cols_sb", [C, 1])
        slope_rows_sb = sb("slope_rows_sb", [P, HEADS])
        distance_sb = sb("distance_sb", [P, CHUNK])
        causal_sb = sb("causal_sb", [P, CHUNK])
        position_sb = sb("position_sb", [C, CHUNK])
        to_end_sb = sb("to_end_sb", [P, 1])
        same_head_sb = sb("same_head_sb", [C, C])
        decay_mask = sb("decay_mask", [P, HEADS, CHUNK])
        q_decay = sb("q_decay", [C, CHUNK])
        k_decay = sb("k_decay", [P, HEADS])
        chunk_decay = sb("chunk_decay", [C, 1])
        wg_sb = sb("wg_sb", [P, EXPERTS])
        wg_part = sb("wg_part", [P, 2 * EXPERTS], F32R)
        bg_sb = sb("bg_sb", [P, EXPERTS])
        numbers_sb = sb("numbers_sb", [P, EXPERTS])
        w1_sb = sb("w1_sb", [P, EXPERTS * HALVES, P])
        w1_part = [sb(f"w1_part{n}", [P, EXPERTS * HALVES, P], F32R) for n in range(2)]
        b1_sb = sb("b1_sb", [P, EXPERTS * HALVES])
        w2_sb = sb("w2_sb", [P, EXPERTS * HALVES, C])
        b2_sb = sb("b2_sb", [P, PAIRS])
        minus_half = sb("minus_half", [P, TILES])
        eps = sb("eps", [P, TILES])
        warm = sb("warm", [P, 1])

        xin = [sb(f"xin{s}", [P, TILES, CHUNK]) for s in range(2)]
        feat = [[sb(f"feat{s}{n}", [P, GT]) for n in range(2)] for s in range(2)]
        embed_T = sb("embed_T", [P, GT])
        h = [sb(f"h{s}", [P, TILES, C]) for s in range(2)]
        h_plus = [sb(f"h_plus{s}", [P, TILES, C]) for s in range(2)]
        stats = [sb(f"stats{n}", [P, TILES, 6]) for n in range(2)]
        moments = [sb(f"moments{n}", [P, TILES, 2]) for n in range(2)]
        rstd = [sb(f"rstd{n}", [P, TILES]) for n in range(2)]
        normed = [sb(f"normed{n}", [P, TILES, 2, C]) for n in range(2)]
        xs = sb("xs", [P, GT], F32R)
        qk_part = sb("qk_part", [P, 3, GT], BF16)
        qk_rest = sb("qk_rest", [P, GT])
        q_stack = [sb(f"q_stack{s}", [STACK, HEADS, GT], BF16) for s in range(2)]
        k_stack = [sb(f"k_stack{s}", [STACK, HEADS, GT], BF16) for s in range(2)]
        q_dec = [sb(f"q_dec{s}", [C, TILES, CHUNK]) for s in range(2)]
        k_dec = [sb(f"k_dec{s}", [P, TILES, C]) for s in range(2)]
        kv_low = sb("kv_low", [P, TILES, 2 * C])
        kv = [sb(f"kv{s}", [P, TILES, 2 * C]) for s in range(2)]
        v_pad = [sb(f"v_pad{s}", [P, TILES, HEADS, 4 * D]) for s in range(2)]

        probs = [sb(f"probs{b}", [P, HEADS, CHUNK]) for b in range(TILES)]
        heads_T = sb("heads_T", [P, 2, CHUNK])
        state = sb("state", [C, IMAGES, C])
        state_new = sb("state_new", [C, TILES, C])
        h2 = [sb(f"h2{s}", [P, TILES, C]) for s in range(2)]
        xs2 = [sb(f"xs2{s}", [P, GT], F32R) for s in range(2)]

        gate_a = sb("gate_a", [P, TILES, EXPERTS])
        gate = sb("gate", [P, TILES, EXPERTS])
        top = sb("top", [P, TILES, 8])
        top_at = sb("top_at", [P, TILES, 8], U32)
        top_gap = sb("top_gap", [P, TILES])
        top_tanh = sb("top_tanh", [P, TILES])
        top_w = sb("top_w", [P, 2, TILES])
        is_top = [sb(f"is_top{n}", [P, TILES, EXPERTS]) for n in range(2)]
        top_part = [sb(f"top_part{n}", [P, TILES, EXPERTS]) for n in range(2)]
        expert_w = [sb(f"expert_w{s}", [P, TILES, EXPERTS]) for s in range(2)]
        hidden = [sb(f"hidden{n}", [P, GT]) for n in range(4)]
        y_T = [sb(f"y_T{n}", [P, GT]) for n in range(2)]
        weighted = [sb(f"weighted{n}", [P, TILES, 2, C]) for n in range(2)]
        acc = [sb(f"acc{s}", [P, TILES, C]) for s in range(2)]

        def bank(name):
            return ctx.enter_context(nc.psum_tensor(name, [P, 512], F32))

        up_ps = [bank("up_ps0"), bank("up_ps1")]
        down_ps = bank("down_ps")
        token_ps = bank("token_ps")
        score_ps = [bank("score_ps0"), bank("score_ps1")]
        att_ps = bank("att_ps")
        front_ps = bank("front_ps")

        kv_ps = score_ps

        loaded_first = sem("loaded_first")
        loaded = sem("loaded")
        loaded_late = sem("loaded_late")
        setup_v = sem("setup_v")
        setup_s = sem("setup_s")
        setup_p = sem("setup_p")
        setup_t = sem("setup_t")
        x_loaded = [sem(f"x_loaded{s}") for s in range(2)]
        stacked = [sem(f"stacked{s}") for s in range(2)]
        stored = [sem(f"stored{s}") for s in range(2)]
        tanh_done = sem("tanh_done")
        silu_done = sem("silu_done")
        embed_ready = sem("embed_ready")
        embed_copied = sem("embed_copied")
        embed_turned = sem("embed_turned")
        h_done = sem("h_done")
        stats_done = [sem("stats_done0"), sem("stats_done1")]
        moments_done = [sem("moments_done0"), sem("moments_done1")]
        var_done = [sem("var_done0"), sem("var_done1")]
        rstd_done = [sem("rstd_done0"), sem("rstd_done1")]
        normed_done = [sem("normed_done0"), sem("normed_done1")]
        turned = [sem("turned0"), sem("turned1")]
        xs_high = [sem("xs_high0"), sem("xs_high1")]
        xs_done = [sem("xs_done0"), sem("xs_done1")]
        h_plus_done = sem("h_plus_done")
        qk_ready = sem("qk_ready")
        part_high = sem("part_high")
        rest_done = sem("rest_done")
        q_dec_done = sem("q_dec_done")
        part_mid = sem("part_mid")
        part_low = sem("part_low")
        kv_ready = sem("kv_ready")
        kv_low_done = sem("kv_low_done")
        kv_done = sem("kv_done")
        k_dec_done = sem("k_dec_done")
        v_pad_done = sem("v_pad_done")
        scores_ready = sem("scores_ready")
        probs_done = sem("probs_done")
        heads_ready = sem("heads_ready")
        heads_copied = sem("heads_copied")
        proj_ready = sem("proj_ready")
        h2_done = sem("h2_done")
        outer_ready = sem("outer_ready")
        outer_masked = sem("outer_masked")
        state_done = sem("state_done")
        gate_ready = sem("gate_ready")
        gate_step = sem("gate_step")
        top_tanh_done = sem("top_tanh_done")
        up_ready = sem("up_ready")
        gelu_done = sem("gelu_done")
        down_done = sem("down_done")
        y_copied = sem("y_copied")
        y_turned = sem("y_turned")
        weighted_done = sem("weighted_done")
        acc_done = sem("acc_done")

        GATE = 10
        SETUP_P = 3
        SETUP_V = 6

        block = ctx.enter_context(nc.Block())

        def values(eng, *counts):
            return [n if isinstance(n, int) else eng.compute_val(n) for n in counts]

        def steps(eng, step):
            for c in range(LEAD):
                step(Turn(None, c))
            with eng.Fori(0, LOOPS) as i:
                for c in range(LEAD, LEAD + 2):
                    step(Turn(i, c))
            for c in range(LEAD + 2 * LOOPS, GROUPS + 3):
                step(Turn(None, c))

        first_loads = [
            (front_scale_sb, front_scale), (front_w_sb, front_w), (front_b_sb, front_bias), (ident, identity),
        ]
        loads = [
            (slope_rows_sb, slope_rows), (slope_cols_sb, slope_cols), (distance_sb, distance),
            (position_sb, position), (to_end_sb, to_end), (wqk_sb, wqk), (wkv_sb, wkv), (causal_sb, causal),
            (bproj_sb, bproj),
        ]
        late_loads = [
            (w1_sb, w1), (wg_sb, wg), (same_head_sb, same_head), (wproj_sb, wproj), (bg_sb, bg),
            (numbers_sb, expert_numbers), (b1_sb, b1), (b2_sb, b2), (w2_sb, w2),
        ]
        ALL_FIRST = 16 * len(first_loads)
        ALL_LOADED = 16 * len(loads)
        ALL_LATE = 16 * len(late_loads)

        @block.sync
        def _(sp):
            def load_x(u):
                if u.back(2).exists:
                    tanhs, silus = values(sp, u.back(2).count(2), u.back(2).count(1))
                    sp.wait_ge(tanh_done, tanhs)
                    sp.wait_ge(silu_done, silus)
                src = x[TILES * u.slot:TILES * (u.slot + 1), :, bass.ds(u.chunk * CHUNK, CHUNK)]
                for half in range(2):
                    sp.dma_start(xin[u.slot][C * half:C * (half + 1), :, :],
                                 src.rearrange("b c t -> c b t")).then_inc(x_loaded[u.slot], 16)

            def stack(u):
                high, mid, low, scored = values(sp, u.count(1), u.count(1), u.count(1), u.back(2).count(8))
                if u.back(2).exists:
                    sp.wait_ge(scores_ready, scored)
                for part, written, count in ((0, part_high, high), (1, part_mid, mid), (2, part_low, low)):
                    sp.wait_ge(written, count)
                    for rows, stacks, parts in ((0, q_stack, Q_PARTS), (C, k_stack, K_PARTS)):
                        for m in range(len(parts)):
                            if parts[m] == part:
                                sp.dma_start(stacks[u.slot][m * D:(m + 1) * D, :, :], qk_part[rows:rows + C, part, :])\
                                    .then_inc(stacked[u.slot], 16)

            def store(w):
                sp.wait_ge(acc_done, w.count(8))
                dst = out[TILES * w.slot:TILES * (w.slot + 1), bass.ds(w.chunk * CHUNK, CHUNK), :]
                sp.dma_start(dst.rearrange("b t c -> t b c"), acc[w.slot][:, :, :]).then_inc(stored[w.slot], 16)

            def step(u):
                if u.ahead(2).exists:
                    load_x(u.ahead(2))
                if u.back(3).exists:
                    store(u.back(3))
                if u.exists:
                    stack(u)

            load_x(Turn(None, 0))
            for dst, src in first_loads:
                sp.dma_start(dst[:], src).then_inc(loaded_first, 16)
            for dst, src in loads:
                sp.dma_start(dst[:], src).then_inc(loaded, 16)
            load_x(Turn(None, 1))
            for dst, src in late_loads:
                sp.dma_start(dst[:], src).then_inc(loaded_late, 16)
            steps(sp, step)
            for s in range(2):
                sp.wait_ge(stored[s], 16 * GROUPS // 2)

        @block.gpsimd
        def _(pool):
            gp = nc.gpsimd
            gp.memset(minus_half[:], -0.5)
            gp.memset(eps[:], EPS)
            gp.memset(spline_rows[:], 1.0).then_inc(setup_p, 1)
            pool.wait_ge(setup_p, 1)
            gp.memset(spline_rows[0:C, 0:1], 0.0).then_inc(setup_p, 1)
            pool.wait_ge(setup_p, 2)
            gp.memset(state[:], 0.0)
            for s in range(2):
                gp.memset(v_pad[s][:], 0.0)
            gp.memset(warm[:], 0.0).then_inc(setup_p, 1)
            pool.wait_ge(setup_p, SETUP_P)

            def rsqrt(n, u):
                pool.wait_ge(moments_done[n], u.count(1))
                if u.back(1).exists:
                    pool.wait_ge(normed_done[n], u.back(1).count(1))
                gp.tensor_tensor(rstd[n][:, :], moments[n][:, :, 1], eps[:, :], ALU.add)\
                    .then_inc(var_done[n], 1)
                pool.wait_ge(var_done[n], u.count(1))
                gp.tensor_tensor(rstd[n][:, :], rstd[n][:, :], minus_half[:, :], ALU.pow)\
                    .then_inc(rstd_done[n], 1)

            def residual(u):
                pool.wait_ge(h_done, u.count(1))
                if u.back(2).exists:
                    pool.wait_ge(h2_done, u.back(2).count(1))
                gp.tensor_tensor(h_plus[u.slot][:, :, :], h[u.slot][:, :, :],
                                 bproj_sb[:, :].unsqueeze(1).to_broadcast([P, TILES, C]), ALU.add)\
                    .then_inc(h_plus_done, 1)

            def low_parts(u):
                pool.wait_ge(part_mid, u.count(1))
                gp.tensor_tensor(qk_part[:, 2, :], qk_rest[:, :], qk_part[:, 1, :], ALU.subtract)\
                    .then_inc(part_low, 1)

            def pad_v(u):
                summed, used = values(pool, u.count(2), u.back(2).count(2))
                pool.wait_ge(loaded, ALL_LOADED)
                pool.wait_ge(kv_done, summed)
                if u.back(2).exists:
                    pool.wait_ge(heads_ready, used)
                for b in range(TILES):
                    for a in range(2):
                        dst = v_pad[u.slot][:, b, 4 * a:4 * a + 4, :].rearrange("p r k -> p (r k)")
                        last = gp.tensor_copy(
                            bass.AP(dst.tensor, dst.offset, [list(dst.ap[0]), [5 * D, 4], [1, D]]),
                            kv[u.slot][:, b, C + 4 * D * a:C + 4 * D * (a + 1)].rearrange("p (r k) -> p r k", r=4))
                    last.then_inc(v_pad_done, 1)

            def add_experts(w, p):
                pool.wait_ge(weighted_done, w.count(4, p + 1))
                for e in range(2):
                    n = 2 * p + e
                    if n == 0:
                        if w.back(2).exists:
                            pool.wait_ge(stored[w.slot], w.back(2).slot_count(16))
                        before = h2[w.slot][:, :, :]
                    else:
                        pool.wait_ge(acc_done, w.count(8, n))
                        before = acc[w.slot][:, :, :]
                    gp.tensor_tensor(acc[w.slot][:, :, :], before, weighted[p % 2][:, :, e, :], ALU.add)\
                        .then_inc(acc_done, 1)

            pool.wait_ge(loaded, ALL_LOADED)

            def step(u):
                att, ffn, old = u.back(1), u.back(2), u.back(3)
                if att.exists:
                    pad_v(att)
                if old.exists:
                    add_experts(old, 2)
                    add_experts(old, 3)
                if u.exists:
                    rsqrt(0, u)
                    residual(u)
                if ffn.exists:
                    add_experts(ffn, 0)
                if u.exists:
                    low_parts(u)
                if att.exists:
                    rsqrt(1, att)
                if ffn.exists:
                    add_experts(ffn, 1)

            steps(pool, step)

        @block.scalar
        def _(act):
            sc = nc.scalar
            def tanh(u, n):
                if n == 0:
                    act.wait_ge(x_loaded[u.slot], u.slot_count(32))
                    if u.back(2).exists:
                        act.wait_ge(embed_ready, u.back(2).count(1))
                sc.activation(feat[u.slot][n][:, :], xin[u.slot][:, :, :].rearrange("c b t -> c (b t)"),
                              ACT.Tanh, scale=front_scale_sb[:, n:n + 1]).then_inc(tanh_done, 1)

            def copy_embed(u):
                act.wait_ge(embed_ready, u.count(1))
                if u.back(1).exists:
                    act.wait_ge(embed_turned, u.back(1).count(1))
                sc.activation(embed_T[:, :], front_ps[:, :], ACT.Identity, bias=embed_bias[:, 0:1])\
                    .then_inc(embed_copied, 1)

            def high_xs(n, u):
                act.wait_ge(turned[n], u.count(1))
                if n == 0:
                    if u.back(1).exists:
                        act.wait_ge(kv_ready, u.back(1).count(1))
                    sc.activation(xs[:, :], front_ps[:, :], ACT.Copy).then_inc(xs_high[0], 1)
                else:
                    if u.back(2).exists:
                        act.wait_ge(gate_ready, u.back(2).count(1))
                        act.wait_ge(up_ready, u.back(2).count(16))
                    sc.activation(xs2[u.slot][:, :], att_ps[:, :], ACT.Copy).then_inc(xs_high[1], 1)

            def high_parts(u):
                act.wait_ge(qk_ready, u.count(1))
                if u.back(1).exists:
                    act.wait_ge(stacked[u.back(1).slot], u.back(1).slot_count(12 * 16))
                sc.activation(qk_part[:, 0, :], front_ps[:, :], ACT.Copy).then_inc(part_high, 1)

            def mid_parts(u):
                act.wait_ge(rest_done, u.count(1))
                sc.activation(qk_part[:, 1, :], qk_rest[:, :], ACT.Copy).then_inc(part_mid, 1)

            def copy_kv_low(u):
                act.wait_ge(kv_ready, u.count(1))
                if u.back(1).exists:
                    act.wait_ge(kv_done, u.back(1).count(2))
                for n in range(2):
                    parts = kv_ps[n][:, :].rearrange("p (b n k) -> p b n k", b=2, n=2)
                    sc.activation(kv_low[:, 2 * n:2 * n + 2, :], parts[:, :, 1, :], ACT.Copy).then_inc(kv_low_done, 1)

            def copy_heads(a):
                act.wait_ge(heads_ready, a.count(2))
                if a.back(1).exists:
                    act.wait_ge(proj_ready, a.back(1).count(1))
                sc.activation(heads_T[:, :, :].rearrange("p a t -> p (a t)"), att_ps[:, 0:2 * CHUNK], ACT.Copy)\
                    .then_inc(heads_copied, 1)

            def gate_tanh(w):
                act.wait_ge(gate_step, w.count(GATE, 4))
                sc.activation(top_tanh[:, :], top_gap[:, :], ACT.Tanh, scale=0.5).then_inc(top_tanh_done, 1)

            def gelus(w, j):
                for k in range(2):
                    n = 2 * j + k
                    act.wait_ge(up_ready, w.count(16, n + 1))
                    if j >= 2 or w.back(1).exists:
                        act.wait_ge(down_done, w.count(8, j - 1))
                    chunk = chunk_of(n)
                    sc.activation(hidden[n % 4][:, :], up_ps[n % 2][:, :], ACT.Gelu, bias=b1_sb[:, chunk:chunk + 1])\
                        .then_inc(gelu_done, 1)

            def copy_y(w, p):
                act.wait_ge(down_done, w.count(8, 2 * p + 2))
                if p >= 2 or w.back(1).exists:
                    act.wait_ge(y_turned, w.count(4, p - 1))
                sc.activation(y_T[p % 2][:, :], down_ps[:, :], ACT.Identity, bias=b2_sb[:, p:p + 1])\
                    .then_inc(y_copied, 1)

            act.wait_ge(setup_v, 1)
            tanh(Turn(None, 0), 0)
            tanh(Turn(None, 0), 1)
            act.wait_ge(setup_v, 2)
            copy_embed(Turn(None, 0))
            act.wait_ge(setup_v, 3)
            for hd in range(HEADS):
                sc.activation(decay_mask[:, hd, :], distance_sb[:, :], ACT.Exp, scale=slope_rows_sb[:, hd:hd + 1])
            sc.activation(q_decay[:, :], position_sb[:, :], ACT.Exp, scale=slope_cols_sb[:, 0:1])
            sc.activation(k_decay[:, :], slope_rows_sb[:, :], ACT.Exp, scale=to_end_sb[:, 0:1])
            sc.activation(chunk_decay[:, :], slope_cols_sb[:, :], ACT.Exp, scale=float(CHUNK)).then_inc(setup_s, 1)
            act.wait_ge(setup_p, SETUP_P)
            act.wait_ge(setup_s, 1)
            sc.activation(warm[:, :], warm[:, :], ACT.Gelu).then_inc(setup_s, 1)

            def step(u):
                a, w, new = u.back(1), u.back(2), u.ahead(1)
                if u.i is None and u.c == 1:
                    act.wait_ge(loaded_late, ALL_LATE)
                for j in range(8):
                    if w.exists:
                        gelus(w, j)
                        if j in (2, 4, 6):
                            copy_y(w, j // 2 - 1)
                    if j == 3 and u.exists:
                        high_xs(0, u)
                    if j == 3 and w.exists:
                        gate_tanh(w)
                    if j == 4 and u.exists:
                        high_parts(u)
                    if j == 4 and a.exists:
                        copy_heads(a)
                    if j == 5 and u.exists:
                        mid_parts(u)
                    if j in (5, 7) and new.exists:
                        tanh(new, j // 2 - 2)
                if a.exists:
                    high_xs(1, a)
                if w.exists:
                    copy_y(w, 3)
                if new.exists:
                    copy_embed(new)
                if u.exists:
                    copy_kv_low(u)

            steps(act, step)

        @block.vector
        def _(dve):
            ve = nc.vector

            def bc(ap, n, k):
                return ap.unsqueeze(1).to_broadcast([ap.shape[0], n, k])

            def silu(u):
                f, x_rows = feat[u.slot][0][0:C, :], xin[u.slot][0:C, :, :].rearrange("c b t -> c (b t)")
                dve.wait_ge(tanh_done, u.count(2, 1))
                ve.scalar_tensor_tensor(f, f, 1.0, x_rows, ALU.add, ALU.mult).then_inc(silu_done, 1)

            split = (((wqk_part[0][:, :], wqk_part[1][:, :]), wqk_sb), ((wkv_parts[:, 0, :], wkv_parts[:, 1, :]), wkv_sb))
            dve.wait_ge(loaded_first, ALL_FIRST)
            ve.tensor_scalar(front_scale_sb[:, :], front_scale_sb[:, :], 0.5, None, ALU.mult)
            ve.tensor_scalar(front_w_sb[:, :, :], front_w_sb[:, :, :], 0.5, None, ALU.mult).then_inc(setup_v, 1)
            dve.wait_ge(setup_t, 1)
            ve.tensor_tensor(embed_bias[:, :], front_b_sb[:, :], front_ps[:, 0:1], ALU.add).then_inc(setup_v, 1)
            silu(Turn(None, 0))
            dve.wait_ge(loaded, ALL_LOADED)
            ve.tensor_scalar(slope_cols_sb[:, :], slope_cols_sb[:, :], -1.0, None, ALU.mult)
            ve.tensor_scalar(slope_rows_sb[:, :], slope_rows_sb[:, :], -1.0, None, ALU.mult).then_inc(setup_v, 1)
            for part, whole in split:
                last = ve.tensor_copy(part[0], whole[:, :])
            last.then_inc(setup_v, 1)
            dve.wait_ge(setup_v, 4)
            for part, whole in split:
                last = ve.tensor_tensor(part[1], whole[:, :], part[0].bitcast(F32), ALU.subtract)
            last.then_inc(setup_v, 1)
            def scale_decays():
                dve.wait_ge(setup_s, 1)
                ve.tensor_scalar(q_decay[:, :], q_decay[:, :], SCALE, None, ALU.mult)
                ve.tensor_tensor(decay_mask[:, :, :], decay_mask[:, :, :], bc(causal_sb[:, :], HEADS, CHUNK),
                                 ALU.mult).then_inc(setup_v, 1)
                dve.wait_ge(setup_v, SETUP_V)

            def split_expert_weights(e):
                w1_high, w1_low = (part[:, HALVES * e:HALVES * (e + 1), :] for part in w1_part)
                if e == 0:
                    dve.wait_ge(loaded_late, ALL_LATE)
                    ve.tensor_copy(wg_part[:, 0:EXPERTS], wg_sb[:, :])
                ve.tensor_copy(w1_high, w1_sb[:, HALVES * e:HALVES * (e + 1), :]).then_inc(setup_v, 1)
                dve.wait_ge(setup_v, SETUP_V + 2 * e + 1)
                if e == 0:
                    ve.tensor_tensor(wg_part[:, EXPERTS:2 * EXPERTS], wg_sb[:, :],
                                     wg_part[:, 0:EXPERTS].bitcast(F32), ALU.subtract)
                ve.tensor_tensor(w1_low, w1_sb[:, HALVES * e:HALVES * (e + 1), :], w1_high.bitcast(F32), ALU.subtract)\
                    .then_inc(setup_v, 1)

            def layer_norm_moments(n, u, src):
                for b in range(TILES):
                    last = ve.bn_stats(stats[n][:, b, :], src[:, b, :])
                last.then_inc(stats_done[n], 1)
                summed, = values(dve, u.count(1))
                dve.wait_ge(loaded, ALL_LOADED)
                dve.wait_ge(stats_done[n], summed)
                for b in range(TILES):
                    last = ve.bn_aggr(moments[n][:, b, :], stats[n][:, b, :])
                last.then_inc(moments_done[n], 1)

            def layer_norm(n, u, src):
                dve.wait_ge(rstd_done[n], u.count(1))
                if u.back(1).exists:
                    dve.wait_ge(turned[n], u.back(1).count(1))
                for b in range(TILES):
                    last = ve.tensor_scalar(normed[n][:, b, :, :], bc(src[:, b, :], 2, C),
                                            moments[n][:, b, 0:1], rstd[n][:, b:b + 1], ALU.subtract, ALU.mult)
                last.then_inc(normed_done[n], 1)

            def embed(u):
                dve.wait_ge(embed_turned, u.count(1))
                ve.tensor_reduce(h[u.slot][:, :, :], front_ps[:, :].rearrange("p (b n c) -> p b c n", b=TILES, n=2),
                                 mybir.AxisListType.X, ALU.add).then_inc(h_done, 1)
                dve.wait_ge(h_done, u.count(1))
                layer_norm_moments(0, u, h[u.slot])

            def low_xs(n, u):
                dve.wait_ge(xs_high[n], u.count(1))
                to, ps = (xs, front_ps) if n == 0 else (xs2[u.slot], att_ps)
                ve.tensor_tensor(to[C:P, :], ps[C:P, :], to[C:P, :].bitcast(F32), ALU.subtract)\
                    .then_inc(xs_done[n], 1)

            def split_qk(u):
                dve.wait_ge(part_high, u.count(1))
                if u.back(1).exists:
                    dve.wait_ge(part_low, u.back(1).count(1))
                ve.tensor_tensor(qk_rest[:, :], front_ps[:, :], qk_part[:, 0, :], ALU.subtract).then_inc(rest_done, 1)
                if u.back(2).exists:
                    dve.wait_ge(heads_ready, u.back(2).count(2))
                ve.tensor_tensor(q_dec[u.slot][:, :, :], front_ps[0:C, :].rearrange("p (b t) -> p b t", b=TILES),
                                 bc(q_decay[:, :], TILES, CHUNK), ALU.mult).then_inc(q_dec_done, 1)

            def add_kv(u):
                for n in range(2):
                    dve.wait_ge(kv_low_done, u.count(2, n + 1))
                    if n == 0 and u.back(2).exists:
                        dve.wait_ge(outer_ready, u.back(2).count(1))
                        dve.wait_ge(v_pad_done, u.back(2).count(4))
                    parts = kv_ps[n][:, :].rearrange("p (b n k) -> p b n k", b=2, n=2)
                    ve.tensor_tensor(kv[u.slot][:, 2 * n:2 * n + 2, :], parts[:, :, 0, :], kv_low[:, 2 * n:2 * n + 2, :],
                                     ALU.add).then_inc(kv_done, 1)

            def decay_k(u):
                dve.wait_ge(kv_done, u.count(2))
                ve.tensor_tensor(k_dec[u.slot][:, :, :].rearrange("p b (d h) -> p b d h", h=HEADS),
                                 kv[u.slot][:, :, 0:C].rearrange("p b (d h) -> p b d h", h=HEADS),
                                 k_decay[:, :].unsqueeze(1).unsqueeze(1).to_broadcast([P, TILES, D, HEADS]), ALU.mult)\
                    .then_inc(k_dec_done, 1)

            def mask_scores(a, b):
                for half in range(2):
                    dve.wait_ge(scores_ready, a.count(8, 2 * b + half + 1))
                    if a.back(1).exists:
                        dve.wait_ge(heads_ready, a.back(1).count(2))
                    ve.tensor_tensor(probs[b][:, 4 * half:4 * half + 4, :],
                                     score_ps[half][:, :].rearrange("p (h t) -> p h t", h=4),
                                     decay_mask[:, 4 * half:4 * half + 4, :], ALU.mult).then_inc(probs_done, 1)

            def add_attention(a):
                dve.wait_ge(proj_ready, a.count(1))
                dve.wait_ge(h_plus_done, a.count(1))
                if a.back(2).exists:
                    dve.wait_ge(acc_done, a.back(2).count(8, 1))
                ve.tensor_tensor(h2[a.slot][:, :, :], att_ps[:, 0:TILES * C].rearrange("p (b c) -> p b c", b=TILES),
                                 h_plus[a.slot][:, :, :], ALU.add).then_inc(h2_done, 1)
                dve.wait_ge(h2_done, a.count(1))
                layer_norm_moments(1, a, h2[a.slot])

            def carry_state(a):
                dve.wait_ge(outer_ready, a.count(1))
                ve.tensor_tensor(state_new[:, :, :], front_ps[0:C, 0:TILES * C].rearrange("p (b c) -> p b c", b=TILES),
                                 bc(same_head_sb[:, :], TILES, C), ALU.mult).then_inc(outer_masked, 1)
                dve.wait_ge(outer_masked, a.count(1))
                dve.wait_ge(heads_ready, a.count(2))
                own = state[:, TILES * a.slot:TILES * (a.slot + 1), :]
                ve.scalar_tensor_tensor(own, own, chunk_decay[:, 0:1], state_new[:, :, :], ALU.mult, ALU.add)\
                    .then_inc(state_done, 1)

            def top_two(w):
                dve.wait_ge(gate_ready, w.count(1))
                both = token_ps[:, 0:TILES * 2 * EXPERTS].rearrange("p (b k) -> p b k", b=TILES)
                ve.tensor_tensor(gate_a[:, :, :], both[:, :, 0:EXPERTS], bc(bg_sb[:, :], TILES, EXPERTS), ALU.add)\
                    .then_inc(gate_step, 1)
                dve.wait_ge(gate_step, w.count(GATE, 1))
                ve.tensor_tensor(gate[:, :, :], gate_a[:, :, :], both[:, :, EXPERTS:2 * EXPERTS], ALU.add)\
                    .then_inc(gate_step, 1)
                summed, = values(dve, w.count(GATE, 2))
                dve.wait_ge(loaded, ALL_LOADED)
                dve.wait_ge(gate_step, summed)
                for b in range(TILES):
                    last = ve.max(top[:, b, :], gate[:, b, :])
                last.then_inc(gate_step, 1)
                dve.wait_ge(gate_step, w.count(GATE, 3))
                ve.tensor_tensor(top_gap[:, :], top[:, :, 0], top[:, :, 1], ALU.subtract).then_inc(gate_step, 1)
                for b in range(TILES):
                    last = ve.max_index(top_at[:, b, :], top[:, b, :], gate[:, b, :])
                last.then_inc(gate_step, 1)

            def weigh_top(w):
                dve.wait_ge(gate_step, w.count(GATE, 5))
                dve.wait_ge(top_tanh_done, w.count(1))
                for n in range(2):
                    ve.tensor_scalar(top_w[:, n, :], top_tanh[:, :], 0.5 - n, 0.5, ALU.mult, ALU.add)
                    last = ve.tensor_tensor(is_top[n][:, :, :], bc(numbers_sb[:, :], TILES, EXPERTS),
                                            top_at[:, :, n:n + 1].to_broadcast([P, TILES, EXPERTS]), ALU.is_equal)
                    last.then_inc(gate_step, 1)
                dve.wait_ge(gate_step, w.count(GATE, 7))
                for n in range(2):
                    ve.tensor_tensor(top_part[n][:, :, :], is_top[n][:, :, :],
                                     top_w[:, n, :].unsqueeze(2).to_broadcast([P, TILES, EXPERTS]), ALU.mult)\
                        .then_inc(gate_step, 1)
                dve.wait_ge(gate_step, w.count(GATE, 9))
                ve.tensor_tensor(expert_w[w.slot][:, :, :], top_part[0][:, :, :], top_part[1][:, :, :], ALU.add)\
                    .then_inc(gate_step, 1)

            def weigh(w, p):
                dve.wait_ge(y_turned, w.count(4, p + 1))
                if p == 0:
                    dve.wait_ge(gate_step, w.count(GATE))
                if p >= 2 or w.back(1).exists:
                    dve.wait_ge(acc_done, w.count(8, 2 * p - 2))
                ve.tensor_tensor(weighted[p % 2][:, :, :, :],
                                 token_ps[:, :].rearrange("p (b e c) -> p b e c", b=TILES, e=2),
                                 expert_w[w.slot][:, :, 2 * p:2 * p + 2].unsqueeze(3).to_broadcast([P, TILES, 2, C]),
                                 ALU.mult).then_inc(weighted_done, 1)

            def step(u):
                a, w, old, new = u.back(1), u.back(2), u.back(3), u.ahead(1)
                for j in range(9):
                    if j == 0 and u.exists and not w.exists:
                        embed(u)
                    if j < 4 and a.exists:
                        mask_scores(a, j)
                    if j == 0 and old.exists:
                        weigh(old, 3)
                    if j == 1 and u.exists and w.exists:
                        embed(u)
                    if j == 2 and u.exists:
                        layer_norm(0, u, h[u.slot])
                    if j == 2 and w.exists:
                        top_two(w)
                    if j == 3 and u.exists:
                        low_xs(0, u)
                    if j == 3 and w.exists:
                        weigh_top(w)
                    if j == 4 and w.exists:
                        weigh(w, 0)
                    if u.i is None and u.c == 0 and j == 3:
                        scale_decays()
                    if j == 4 and u.exists:
                        split_qk(u)
                    if j == 5 and a.exists:
                        add_attention(a)
                    if j == 5 and w.exists:
                        weigh(w, 1)
                    if j == 6 and new.exists:
                        silu(new)
                    if j == 6 and a.exists:
                        layer_norm(1, a, h2[a.slot])
                    if j == 6 and a.exists:
                        carry_state(a)
                    if j == 8 and a.exists:
                        low_xs(1, a)
                    if j == 8 and w.exists:
                        weigh(w, 2)
                    if j == 8 and u.exists:
                        add_kv(u)
                        decay_k(u)
                    if u.i is None and u.c == 1 and j < EXPERTS:
                        split_expert_weights(j)

            steps(dve, step)

        @block.tensor
        def _(pe):
            te = nc.tensor
            pe.wait_ge(loaded_first, ALL_FIRST)
            pe.wait_ge(setup_p, SETUP_P)
            pe.wait_ge(setup_v, 1)
            for n in range(2):
                last = te.matmul(front_ps[C * n:C * (n + 1), 0:1], front_w_sb[:, n, :], spline_rows[:, n:n + 1],
                                 start=True, stop=True)
            last.then_inc(setup_t, 1)
            pe.wait_ge(setup_v, 2)

            def up(w, j):
                for k in range(2):
                    n = 2 * j + k
                    if n == 0:
                        pe.wait_ge(xs_done[1], w.count(1))
                    if n >= 2 or w.back(1).exists:
                        pe.wait_ge(gelu_done, w.count(16, n - 1))
                    chunk = chunk_of(n)
                    te.matmul(up_ps[n % 2][:, :], w1_part[0][:, chunk, :], xs2[w.slot][:, :], start=True, stop=False)
                    te.matmul(up_ps[n % 2][:, :], w1_part[1][:, chunk, :], xs2[w.slot][:, :], start=False, stop=True)\
                        .then_inc(up_ready, 1)

            def down(w, j):
                pe.wait_ge(gelu_done, w.count(16, 2 * j + 2))
                if j % 2 == 0 and (j or w.back(1).exists):
                    pe.wait_ge(y_copied, w.count(4, j // 2))
                for k in range(2):
                    n = 2 * j + k
                    last = te.matmul(down_ps[C * k:C * (k + 1), :], w2_sb[:, chunk_of(n), :], hidden[n % 4][:, :],
                                     start=j % 2 == 0, stop=j % 2 == 1)
                last.then_inc(down_done, 1)

            def turn_y(w, p):
                pe.wait_ge(y_copied, w.count(4, p + 1))
                if p == 0:
                    pe.wait_ge(gate_step, w.count(GATE, 2))
                else:
                    pe.wait_ge(weighted_done, w.count(4, p))
                for b in range(TILES):
                    last = te.transpose(token_ps[:, P * b:P * (b + 1)], y_T[p % 2][:, CHUNK * b:CHUNK * (b + 1)],
                                        ident[:, :])
                last.then_inc(y_turned, 1)

            def gate_logits(w):
                if w.back(1).exists:
                    pe.wait_ge(weighted_done, w.back(1).count(4))
                for b in range(TILES):
                    last = te.matmul(token_ps[:, 2 * EXPERTS * b:2 * EXPERTS * (b + 1)],
                                     xs2[w.slot][:, CHUNK * b:CHUNK * (b + 1)], wg_part[:, :], start=True, stop=True)
                last.then_inc(gate_ready, 1)

            def scores(a, b):
                if b == 0:
                    pe.wait_ge(stacked[a.slot], a.slot_count(12 * 16))
                for half in range(2):
                    if b or a.back(1).exists:
                        pe.wait_ge(probs_done, a.count(8, 2 * b + half - 1))
                    if b == 0:
                        pe.wait_ge(kv_done, a.count(2, half + 1))
                    for r in range(4):
                        hd = 4 * half + r
                        cols = slice(CHUNK * b, CHUNK * (b + 1))
                        last = te.matmul(score_ps[half][:, CHUNK * r:CHUNK * (r + 1)], k_stack[a.slot][:, hd, cols],
                                         q_stack[a.slot][:, hd, cols], start=True, stop=True)
                    last.then_inc(scores_ready, 1)

            def heads(a, pair):
                if pair == 0:
                    pe.wait_ge(q_dec_done, a.count(1))
                    if a.back(1).exists:
                        pe.wait_ge(xs_done[1], a.back(1).count(1))
                    if a.back(2).exists:
                        pe.wait_ge(state_done, a.back(2).count(1))
                padded, masked = values(pe, a.count(4, 2 * pair + 2), a.count(8, 4 * pair + 4))
                pe.wait_ge(loaded, ALL_LOADED)
                pe.wait_ge(v_pad_done, padded)
                pe.wait_ge(probs_done, masked)
                cols, tiles = slice(CHUNK * pair, CHUNK * (pair + 1)), (2 * pair, 2 * pair + 1)
                for b in tiles:
                    row = C * (b % 2)
                    te.matmul(att_ps[row:row + C, cols], state[:, TILES * a.slot + b, :], q_dec[a.slot][:, b, :],
                              start=True, stop=False, skip_group_check=True)
                for r in range(4):
                    for b in tiles:
                        for half in range(2):
                            row = C * (b % 2) + 32 * half
                            last = te.matmul(att_ps[row:row + 32, cols], v_pad[a.slot][:, b, 4 * half + r, :],
                                             probs[b][:, 4 * half + r, :], start=False, stop=r == 3,
                                             skip_group_check=True)
                last.then_inc(heads_ready, 1)

            def project(a):
                pe.wait_ge(heads_copied, a.count(1))
                for pair in range(2):
                    last = te.matmul(att_ps[:, P * pair:P * (pair + 1)], heads_T[:, pair, :], wproj_sb[:, :],
                                     start=True, stop=True)
                last.then_inc(proj_ready, 1)

            def turn(n, u):
                pe.wait_ge(normed_done[n], u.count(1))
                ps = front_ps if n == 0 else att_ps
                for b in range(TILES):
                    last = te.transpose(ps[:, CHUNK * b:CHUNK * (b + 1)],
                                        normed[n][:, b, :, :].rearrange("p r c -> p (r c)"), ident[:, :])
                last.then_inc(turned[n], 1)

            def embedding(u):
                pe.wait_ge(tanh_done, u.count(2))
                pe.wait_ge(silu_done, u.count(1))
                if u.back(2).exists:
                    pe.wait_ge(outer_masked, u.back(2).count(1))
                elif u.back(1).exists:
                    pe.wait_ge(part_high, u.back(1).count(1))
                    pe.wait_ge(q_dec_done, u.back(1).count(1))
                for n in range(2):
                    last = te.matmul(front_ps[C * n:C * (n + 1), :], front_w_sb[:, n, :], feat[u.slot][n][:, :],
                                     start=True, stop=True)
                last.then_inc(embed_ready, 1)

            def turn_embed(u):
                pe.wait_ge(embed_copied, u.count(1))
                for b in range(TILES):
                    last = te.transpose(front_ps[:, P * b:P * (b + 1)], embed_T[:, CHUNK * b:CHUNK * (b + 1)],
                                        ident[:, :])
                last.then_inc(embed_turned, 1)

            def project_qk(u):
                pe.wait_ge(xs_done[0], u.count(1))
                for n in range(2):
                    last = te.matmul(front_ps[:, :], wqk_part[n][:, :], xs[:, :], start=n == 0, stop=n == 1)
                last.then_inc(qk_ready, 1)

            def project_kv(u):
                if u.back(1).exists:
                    pe.wait_ge(probs_done, u.back(1).count(8))
                for b in range(TILES):
                    last = te.matmul(kv_ps[b // 2][:, 2 * P * (b % 2):2 * P * (b % 2 + 1)],
                                     xs[:, CHUNK * b:CHUNK * (b + 1)], wkv_parts[:, :, :].rearrange("p n k -> p (n k)"),
                                     start=True, stop=True)
                last.then_inc(kv_ready, 1)

            def outer(a, u):
                pe.wait_ge(k_dec_done, a.count(1))
                if u.exists:
                    pe.wait_ge(part_high, u.count(1))
                    pe.wait_ge(q_dec_done, u.count(1))
                for b in range(TILES):
                    last = te.matmul(front_ps[0:C, C * b:C * (b + 1)], k_dec[a.slot][:, b, :], kv[a.slot][:, b, C:2 * C],
                                     start=True, stop=True)
                last.then_inc(outer_ready, 1)

            def step(u):
                a, w, old, new = u.back(1), u.back(2), u.back(3), u.ahead(1)
                if u.i is None and u.c == 1:
                    pe.wait_ge(loaded_late, ALL_LATE)
                if u.i is None and u.c == 2:
                    pe.wait_ge(setup_v, SETUP_V + 2 * EXPERTS)
                for j in range(9):
                    if j == 0 and u.exists and not w.exists:
                        turn_embed(u)
                    if j == 8 and a.exists:
                        turn(1, a)
                    if w.exists:
                        if j < 8:
                            up(w, j)
                        if j >= 1:
                            down(w, j - 1)
                    if j == 0 and old.exists:
                        turn_y(old, 3)
                    if j <= 3 and a.exists:
                        scores(a, j)
                    if j == 2 and a.exists:
                        heads(a, 0)
                    if j == 1 and u.exists and w.exists:
                        turn_embed(u)
                    if j == 1 and w.exists:
                        gate_logits(w)
                    if j == 3 and u.exists:
                        turn(0, u)
                    if j == 4 and w.exists:
                        turn_y(w, 0)
                    if j == 4 and u.exists:
                        project_qk(u)
                    if j == 4 and a.exists:
                        heads(a, 1)
                    if j == 5 and a.exists:
                        project(a)
                    if j == 5 and w.exists:
                        turn_y(w, 1)
                    if j == 6 and a.exists:
                        outer(a, u)
                    if j == 8 and w.exists:
                        turn_y(w, 2)
                    if j == 8 and new.exists:
                        embedding(new)
                    if j == 8 and u.exists:
                        project_kv(u)

            embedding(Turn(None, 0))
            pe.wait_ge(setup_v, 5)
            steps(pe, step)


def chunk_of(n):
    pair, half, e = n // 4, n % 4 // 2, n % 2
    return (2 * pair + e) * HALVES + half


def kernel(**inputs):
    import numpy as np
    import concourse.bacc as bacc
    from concourse.bass_utils import run_bass_kernel_spmd

    f = {k: np.ascontiguousarray(a) for k, a in inputs.items()}
    twice = lambda a: np.concatenate([a, a], axis=0)
    on_diagonal = lambda a: np.block([[a, np.zeros_like(a)], [np.zeros_like(a), a]])
    rows = lambda a, n=P: np.broadcast_to(a, (n,) + a.shape)
    bases, spline = f["L0_tok_bases"], f["L0_tok_W_spline"].reshape(C, C, 3)
    ones = np.ones((C,), np.float32)
    at = np.arange(CHUNK)
    diff = at[None, :] - at[:, None]
    wq, wk, wv = (f["L0_attn_w_qkv"][:, C * n:C * (n + 1)] for n in range(3))
    wq, wk = (a.reshape(C, HEADS, D).transpose(0, 2, 1).reshape(C, C) for a in (wq, wk))
    host = {
        "x": f["x"].reshape(IMAGES, C, TOKENS),
        "front_w": np.stack([np.concatenate([f["L0_tok_W_base"].T, spline[:, :, 0].T]),
                             np.concatenate([spline[:, :, 1].T, spline[:, :, 2].T])], axis=1),
        "front_scale": np.stack([np.concatenate([ones, bases[:, 0]]),
                                 np.concatenate([bases[:, 1], bases[:, 2]])], axis=1),
        "front_bias": np.concatenate([f["L0_tok_b_base"], f["L0_tok_b_spline"]])[:, None],
        "wqk": twice(np.concatenate([wq, wk], axis=1)),
        "wkv": twice(np.concatenate([wk, wv], axis=1)),
        "wproj": on_diagonal(f["L0_attn_w_proj"]),
        "bproj": rows(f["L0_attn_b_proj"]),
        "slope_cols": np.tile(f["L0_attn_slopes"], D)[:, None],
        "slope_rows": rows(f["L0_attn_slopes"]),
        "wg": twice(f["L0_ffn_Wg"]),
        "bg": rows(f["L0_ffn_bg"]),
        "w1": twice(f["L0_ffn_W1"].transpose(1, 0, 2).reshape(C, EXPERTS * HALVES, P)),
        "b1": f["L0_ffn_b1"].reshape(EXPERTS * HALVES, P).T,
        "w2": f["L0_ffn_W2"].reshape(EXPERTS * HALVES, P, C).transpose(1, 0, 2),
        "b2": f["L0_ffn_b2"].reshape(PAIRS, 2 * C).T,
        "identity": np.eye(P, dtype=np.float32),
        "distance": np.maximum(diff, 0).astype(np.float32),
        "causal": np.where(diff >= 0, SCALE, 0.0).astype(np.float32),
        "position": rows(at.astype(np.float32), C),
        "to_end": (CHUNK - at).astype(np.float32)[:, None],
        "same_head": np.kron(np.tile(np.eye(HEADS), (D, 1)), np.ones((1, D))).astype(np.float32),
        "expert_numbers": rows(np.arange(EXPERTS, dtype=np.float32)),
    }
    host = {k: np.ascontiguousarray(a) for k, a in host.items()}
    nc = bacc.Bacc("TRN2", target_bir_lowering=False, num_devices=1)
    args = {k: nc.dram_tensor(f"in_{k}", a.shape, mybir.dt.from_np(a.dtype), kind="ExternalInput").ap()
            for k, a in host.items()}
    out = nc.dram_tensor("out", (IMAGES, TOKENS, C), F32, kind="ExternalOutput").ap()
    build_tower(nc, **args, out=out)
    r = run_bass_kernel_spmd(nc, [{f"in_{k}": a for k, a in host.items()}], core_ids=[0])
    return r.results[0]["out"]
```
